# Optimizing a Trainium2 kernel written in Bass

```python
import numpy as np
import jax
import jax.numpy as jnp

def _softmax(x, axis=-1):
    return jax.nn.softmax(x, axis=axis)

def _gelu(x):
    return jax.nn.gelu(x, approximate=True)

def _silu(x):
    return jax.nn.silu(x)

def _sigmoid(x):
    return jax.nn.sigmoid(x)

def _layernorm(x, axis=-1, eps=1e-05):
    m = jnp.mean(x, axis=axis, keepdims=True)
    v = jnp.var(x, axis=axis, keepdims=True)
    return (x - m) / jnp.sqrt(v + eps)

def _scatter_add(tgt, idx, src, axis=0):
    return tgt.at[idx].add(src)

def _segment_sum(src, seg, n):
    return jax.ops.segment_sum(src, seg, n)
kernel_name = 'mk_macaron_d1_jaxref_r8_dd4d49'

def setup_inputs(seed: int=0):
    np.random.seed(seed)
    _w = jnp.asarray

    def _L0_attn_setup():
        import jax, jax.numpy as jnp
        import numpy as np
        import math
        NUM_HEADS = 8
        D_HEAD = 128
        DEPTH = 1
        LAMBDA_INIT = 0.8 - 0.6 * math.exp(-0.3 * DEPTH)
        EPS = 1e-05
        key = jax.random.key(seed)
        ks = jax.random.split(key, 10)
        B, N, D = (2, 256, 128)
        s = 0.02
        return {'X': jax.random.normal(ks[0], (B, N, D), jnp.float32), 'Wq': jax.random.normal(ks[1], (2 * D_HEAD * NUM_HEADS, D), jnp.float32) * s, 'Wk': jax.random.normal(ks[2], (2 * D_HEAD * NUM_HEADS, D), jnp.float32) * s, 'Wv': jax.random.normal(ks[3], (2 * D_HEAD * NUM_HEADS, D), jnp.float32) * s, 'Wo': jax.random.normal(ks[4], (D, 2 * D_HEAD * NUM_HEADS), jnp.float32) * s, 'lambda_q1': jax.random.normal(ks[5], (NUM_HEADS, D_HEAD), jnp.float32) * 0.1, 'lambda_k1': jax.random.normal(ks[6], (NUM_HEADS, D_HEAD), jnp.float32) * 0.1, 'lambda_q2': jax.random.normal(ks[7], (NUM_HEADS, D_HEAD), jnp.float32) * 0.1, 'lambda_k2': jax.random.normal(ks[8], (NUM_HEADS, D_HEAD), jnp.float32) * 0.1, 'rms_scale': jnp.ones((2 * D_HEAD,), jnp.float32)}
    _L0_attn_in = _L0_attn_setup()

    def _L0_ffn_setup():
        import jax, jax.numpy as jnp
        import numpy as np
        DIM = 128
        HEADS = 8
        NUM_EXPERTS = 8192
        NUM_KEYS = 32
        DIM_KEY = 64
        TOPK = 16

        def _rmsnorm(v, g):
            scale = jnp.sqrt(jnp.asarray(v.shape[-1], v.dtype))
            n = jnp.maximum(jnp.linalg.norm(v, axis=-1, keepdims=True), 1e-12)
            return v / n * g * scale
        key = jax.random.key(seed)
        ks = jax.random.split(key, 6)
        B, N = (2, 64)
        x = jax.random.normal(ks[0], (B, N, DIM), dtype=jnp.float32)
        gamma = jnp.ones((DIM,), dtype=jnp.float32)
        wq = jax.random.normal(ks[1], (2 * HEADS * DIM_KEY, DIM), dtype=jnp.float32) * 0.02
        keys = jax.random.normal(ks[2], (HEADS, NUM_KEYS, 2, DIM_KEY), dtype=jnp.float32) * 0.02
        table_down = jax.random.normal(ks[3], (NUM_EXPERTS, DIM), dtype=jnp.float32) * 0.02
        table_up = jax.random.normal(ks[4], (NUM_EXPERTS, DIM), dtype=jnp.float32) * 0.02
        return {'x': x, 'gamma': gamma, 'wq': wq, 'keys': keys, 'table_down': table_down, 'table_up': table_up}
    _L0_ffn_in = _L0_ffn_setup()
    _d = {'L0_attn_X': _L0_attn_in['X'], 'L0_attn_Wq': _L0_attn_in['Wq'], 'L0_attn_Wk': _L0_attn_in['Wk'], 'L0_attn_Wv': _L0_attn_in['Wv'], 'L0_attn_Wo': _L0_attn_in['Wo'], 'L0_attn_lambda_q1': _L0_attn_in['lambda_q1'], 'L0_attn_lambda_k1': _L0_attn_in['lambda_k1'], 'L0_attn_lambda_q2': _L0_attn_in['lambda_q2'], 'L0_attn_lambda_k2': _L0_attn_in['lambda_k2'], 'L0_attn_rms_scale': _L0_attn_in['rms_scale'], 'L0_ffn_gamma': _L0_ffn_in['gamma'], 'L0_ffn_wq': _L0_ffn_in['wq'], 'L0_ffn_keys': _L0_ffn_in['keys'], 'L0_ffn_table_down': _L0_ffn_in['table_down'], 'L0_ffn_table_up': _L0_ffn_in['table_up']}
    _x0 = _d['L0_attn_X']
    _d['L0_attn_X'] = jax.random.normal(jax.random.fold_in(jax.random.key(seed), 1), (16, 256, 128), dtype=_x0.dtype)
    del _x0
    return _d

def reference(L0_attn_X, L0_attn_Wq, L0_attn_Wk, L0_attn_Wv, L0_attn_Wo, L0_attn_lambda_q1, L0_attn_lambda_k1, L0_attn_lambda_q2, L0_attn_lambda_k2, L0_attn_rms_scale, L0_ffn_gamma, L0_ffn_wq, L0_ffn_keys, L0_ffn_table_down, L0_ffn_table_up):

    def _L0_attn_ref(X, Wq, Wk, Wv, Wo, lambda_q1, lambda_k1, lambda_q2, lambda_k2, rms_scale):
        import jax, jax.numpy as jnp
        import numpy as np
        import math
        NUM_HEADS = 8
        D_HEAD = 128
        DEPTH = 1
        LAMBDA_INIT = 0.8 - 0.6 * math.exp(-0.3 * DEPTH)
        EPS = 1e-05
        B, N, D = X.shape
        H, dh = (NUM_HEADS, D_HEAD)

        def proj(W):
            y = jnp.einsum('bnd,ed->bne', X, W)
            return y.reshape(B, N, H, 2 * dh).transpose(0, 2, 1, 3)
        Q = proj(Wq)
        K = proj(Wk)
        V = proj(Wv)
        Q1, Q2 = (Q[..., :dh], Q[..., dh:])
        K1, K2 = (K[..., :dh], K[..., dh:])
        lam1 = jnp.exp(jnp.sum(lambda_q1 * lambda_k1, axis=-1))
        lam2 = jnp.exp(jnp.sum(lambda_q2 * lambda_k2, axis=-1))
        lam = (lam1 - lam2 + LAMBDA_INIT)[None, :, None, None]
        scaling = 1.0 / math.sqrt(dh)
        A1 = jnp.einsum('bhqd,bhkd->bhqk', Q1, K1) * scaling
        A2 = jnp.einsum('bhqd,bhkd->bhqk', Q2, K2) * scaling
        attn = jax.nn.softmax(A1, axis=-1) - lam * jax.nn.softmax(A2, axis=-1)
        O = jnp.einsum('bhqk,bhkd->bhqd', attn, V)
        rms = jnp.sqrt(jnp.mean(O * O, axis=-1, keepdims=True) + EPS)
        O = O / rms * rms_scale
        O = O * (1.0 - LAMBDA_INIT)
        O = O.transpose(0, 2, 1, 3).reshape(B, N, H * 2 * dh)
        return jnp.einsum('bne,de->bnd', O, Wo)

    def _L0_ffn_ref(x, gamma, wq, keys, table_down, table_up):
        import jax, jax.numpy as jnp
        import numpy as np
        DIM = 128
        HEADS = 8
        NUM_EXPERTS = 8192
        NUM_KEYS = 32
        DIM_KEY = 64
        TOPK = 16

        def _rmsnorm(v, g):
            scale = jnp.sqrt(jnp.asarray(v.shape[-1], v.dtype))
            n = jnp.maximum(jnp.linalg.norm(v, axis=-1, keepdims=True), 1e-12)
            return v / n * g * scale
        B, N, D = x.shape
        xn = _rmsnorm(x, gamma)
        gate = xn
        q = gate @ wq.T
        q = q.reshape(B, N, 2, HEADS, DIM_KEY).transpose(2, 0, 1, 3, 4)
        sim = jnp.einsum('pbnhd,hkpd->pbnhk', q, keys)
        sx, ix = jax.lax.top_k(sim[0], TOPK)
        sy, iy = jax.lax.top_k(sim[1], TOPK)
        all_scores = (sx[..., :, None] + sy[..., None, :]).reshape(B, N, HEADS, TOPK * TOPK)
        all_indices = (ix[..., :, None] * NUM_KEYS + iy[..., None, :]).reshape(B, N, HEADS, TOPK * TOPK)
        scores, pk = jax.lax.top_k(all_scores, TOPK)
        indices = jnp.take_along_axis(all_indices, pk, axis=-1)
        wd = table_down[indices]
        wu = table_up[indices]
        h = jnp.einsum('bnd,bnhkd->bnhk', xn, wd)
        h = jax.nn.gelu(h, approximate=False) * jax.nn.softmax(scores, axis=-1)
        out = jnp.einsum('bnhk,bnhkd->bnd', h, wu)
        return out
    x = L0_attn_X
    x = x + 0.5 * _L0_ffn_ref(_layernorm(x, axis=-1), L0_ffn_gamma, L0_ffn_wq, L0_ffn_keys, L0_ffn_table_down, L0_ffn_table_up)
    x = x + _L0_attn_ref(_layernorm(x, axis=-1), L0_attn_Wq, L0_attn_Wk, L0_attn_Wv, L0_attn_Wo, L0_attn_lambda_q1, L0_attn_lambda_k1, L0_attn_lambda_q2, L0_attn_lambda_k2, L0_attn_rms_scale)
    x = x + 0.5 * _L0_ffn_ref(_layernorm(x, axis=-1), L0_ffn_gamma, L0_ffn_wq, L0_ffn_keys, L0_ffn_table_down, L0_ffn_table_up)
    return x

_drawn_inputs = setup_inputs


def setup_inputs(seed=0):
    import zlib

    import numpy as np

    out = dict(_drawn_inputs(seed))
    spreads = {'L0_attn_rms_scale': (1.0, 0.2), 'L0_ffn_gamma': (1.0, 0.6)}
    factors = {'L0_attn_lambda_k1': 4.178,
     'L0_attn_lambda_k2': 5.32,
     'L0_ffn_wq': 8.0,
     'L0_ffn_keys': 8.0,
     'L0_ffn_table_down': 8.0,
     'L0_ffn_table_up': 8.0}
    for name, (base, spread) in spreads.items():
        noise = np.random.default_rng([zlib.crc32(name.encode()), seed]).standard_normal(out[name].shape)
        drawn = base * np.exp(spread * noise) if base else spread * noise
        out[name] = jnp.asarray(drawn.astype(out[name].dtype))
    for name, factor in factors.items():
        out[name] = (out[name] * factor).astype(out[name].dtype)
    return out
```

```python
import math
from contextlib import ExitStack

import concourse.bass as bass
from concourse import mybir

F32 = mybir.dt.float32
BF16 = mybir.dt.bfloat16
ALU = mybir.AluOpType
ACT = mybir.ActivationFunctionType
AX = mybir.AxisListType

P = 128
HEADS = 8
DIM_HEAD = 128
KEYS = 32
EXPERTS = KEYS * KEYS
TOPK = 16
EPS = 1e-5
NORM_FLOOR = 1e-12
LAMBDA_INIT = 0.8 - 0.6 * math.exp(-0.3 * 1)
LOWEST = -3.0e38

BLOCKS = [(0, 1, 16), (1, 1, 8), (2, 2, 5), (4, 4, 3), (8, 8, 1)]
CANDS = sum(r * c for _, r, c in BLOCKS)

UNITS = 8
STEPS = 4
HEAD_START = [2, 5, 8, 11, 14, 17, 20, 23]
ATT_STAGES = 10
PE_STAGES = ("normalize", 0, 1, 5, 6, 7, 8)


class Count:

    def __init__(self, j, a, b):
        self.j, self.a, self.b = j, a, b

    def __add__(self, k):
        return Count(self.j, self.a, self.b + k)

    def __sub__(self, k):
        return self + (-k)

    def __mul__(self, k):
        return Count(self.j, self.a * k, self.b * k)

    def odd(self):
        assert self.a % 2 == 0
        return self.b % 2

    def value(self):
        if isinstance(self.j, int):
            return self.a * self.j + self.b
        return self.j * self.a + self.b if self.a else self.b


def reach(engine, sem, count):
    v = count.value() if isinstance(count, Count) else count
    if not isinstance(v, int) or v > 0:
        engine.wait_ge(sem, v)


def build(nc, x, wq16, keysT, gamma, wq_a, wk_a, wv_a, wvT, woT, rms, lam_q, lam_k, downT, up,
          select, ident, out):
    TILES = x.shape[1]
    BATCHES = TILES // 2
    LAST = TILES * 2 - 1
    LOOP = (2, BATCHES - 2)

    ctx = ExitStack()
    with ctx:
        def sb(name, shape, dt=F32):
            return ctx.enter_context(nc.sbuf_tensor(name, shape, dt))

        def ps(name, shape):
            return ctx.enter_context(nc.psum_tensor(name, shape, F32))

        def sem(name):
            return ctx.enter_context(nc.semaphore(name))

        x_all = sb("x_all", [P, TILES, P])
        wq16_sb = sb("wq16_sb", [64, 2 * HEADS, P])
        keys_sb = sb("keys_sb", [64, 2 * HEADS, KEYS])
        gamma_sb = sb("gamma_sb", [P, 1])
        w_sim = sb("w_sim", [P, 2 * HEADS * KEYS])
        down = sb("down", [P, EXPERTS])
        up_sb = sb("up_sb", [P, EXPERTS // P, P])
        select_f = sb("select_f", [P, EXPERTS])
        select_sb = sb("select_sb", [P, EXPERTS], BF16)
        ident_sb = sb("ident_sb", [P, P])
        ident_b = sb("ident_b", [P, P], BF16)
        ones = sb("ones", [P, P])
        wqa_sb = sb("wqa_sb", [P, 2 * HEADS, P])
        wka_sb = sb("wka_sb", [P, 2 * HEADS, P])
        wva_sb = sb("wva_sb", [P, 2 * HEADS, P])
        woT_sb = sb("woT_sb", [P, 2 * HEADS, P])
        rms_sb = sb("rms_sb", [P, 2])
        m_sb = sb("m_sb", [P, 2 * HEADS, P])
        wn_sb = sb("wn_sb", [P, HEADS, 3 * P])
        lamq_sb = sb("lamq_sb", [P, 2 * HEADS])
        lamk_sb = sb("lamk_sb", [P, 2 * HEADS])
        lam_prod = sb("lam_prod", [P, 2 * HEADS])
        lam_exp = sb("lam_exp", [P, 2, HEADS])
        neg_lam = sb("neg_lam", [P, HEADS])
        z = sb("z", [P, P])
        zT = sb("zT", [P, 2, P])
        sim = sb("sim", [P, 2, 2 * HEADS, KEYS])
        high_mid = sb("high_mid", [P, HEADS, 2, 2 * KEYS], BF16)
        rest_mid = sb("rest_mid", [P, HEADS, 2 * KEYS])
        low = sb("low", [P, HEADS, 2 * KEYS], BF16)
        high_midT = sb("high_midT", [P, 2, HEADS, P], BF16)
        lowT = sb("lowT", [P, 2, HEADS // 2, P], BF16)
        stats = sb("stats", [P, 6])
        meanvar = sb("meanvar", [P, 2])
        scale = sb("scale", [P, 3])
        minus_half = sb("minus_half", [P, 2])
        top = sb("top", [P, HEADS, 2, TOPK])
        rest = sb("rest", [P, 2 * HEADS, KEYS])
        cands = sb("cands", [P, HEADS, CANDS])
        cands_a = sb("cands_a", [P, HEADS, CANDS])
        cands_b = sb("cands_b", [P, HEADS, CANDS])
        best = sb("best", [P, HEADS, TOPK])
        best_d = sb("best_d", [P, HEADS, TOPK])
        best_e = sb("best_e", [P, HEADS, TOPK])
        next_best = sb("next_best", [P, HEADS])
        z_sum = sb("z_sum", [P, HEADS])
        z_ln = sb("z_ln", [P, HEADS])
        thr = sb("thr", [P, 2, HEADS])
        bias = sb("bias", [P, 2, HEADS])
        e_buf = sb("e_buf", [P, 2, EXPERTS])
        w_buf = sb("w_buf", [P, 2, EXPERTS])
        p_acc = sb("p_acc", [P, 2, EXPERTS])
        act_h = sb("act_h", [P, 2, EXPERTS])
        g_buf = sb("g_buf", [P, EXPERTS])
        gT = sb("gT", [P, EXPERTS])
        astats = sb("astats", [P, 2, 6])
        ameanvar = sb("ameanvar", [P, 2, 2])
        avar = sb("avar", [P, 2])
        ascale = sb("ascale", [P, 2])
        r_sb = sb("r_sb", [P, 2, P])
        xl = sb("xl", [P, 2, P])
        xlT = sb("xlT", [P, 2 * P])
        t_sb = sb("t_sb", [P, 4 * P])
        row_max = sb("row_max", [P, 4])
        neg_max = sb("neg_max", [P, 4])
        e_att = sb("e_att", [P, 4, 2 * P])
        z_att = sb("z_att", [P, 2, 2])
        rz_att = sb("rz_att", [P, 2, 2, 2])
        mix = sb("mix", [P, 2])
        a_att = sb("a_att", [P, 2, 2 * P])
        aT = sb("aT", [P, 2, 2 * P])
        yT = sb("yT", [P, 2 * P])
        squares = sb("squares", [P, 2, 2 * P])
        sq_sum = sb("sq_sum", [P, 2])
        inv_a = sb("inv_a", [P, 2])
        inv_b = sb("inv_b", [P, 2])
        mean_sq = sb("mean_sq", [P, 2])
        inv_rms = sb("inv_rms", [P, 2])
        out_scale = sb("out_scale", [P, 2])

        s_ps = ps("s_ps", [P, 2, EXPERTS])
        misc = ps("misc", [P, 512])
        misc_b = misc[:, :].bitcast(BF16)
        att_s = ps("att_s", [P, 2, 512])
        att_m = ps("att_m", [P, 512])

        x_in = sem("x_in")
        sim_w_in = sem("sim_w_in")
        tables_in = sem("tables_in")
        consts_in = sem("consts_in")
        att_w_in = sem("att_w_in")
        lam_in = sem("lam_in")
        ones_set = sem("ones_set")
        consts_b = sem("consts_b")
        w_sim_mm = sem("w_sim_mm")
        w_sim_ready = sem("w_sim_ready")
        lam_mul = sem("lam_mul")
        lam_mm = sem("lam_mm")
        lam_exped = sem("lam_exped")
        wo_scaled = sem("wo_scaled")
        m_mm = sem("m_mm")
        m_ready = sem("m_ready")
        n_mm = sem("n_mm")
        n_ready = sem("n_ready")
        half_set = sem("half_set")
        var_ready = sem("var_ready")
        scale_ready = sem("scale_ready")
        z_ready = sem("z_ready")
        zT_mm = sem("zT_mm")
        zT_ready = sem("zT_ready")
        sim_mm = sem("sim_mm")
        sim_ready = sem("sim_ready")
        high_ready = sem("high_ready")
        parts_step = sem("parts_step")
        parts_ready = sem("parts_ready")
        highT_mm = sem("highT_mm")
        highT_ready = sem("highT_ready")
        lowT_mm = sem("lowT_mm")
        lowT_ready = sem("lowT_ready")
        best_d_ready = sem("best_d_ready")
        best_e_ready = sem("best_e_ready")
        z_sum_ready = sem("z_sum_ready")
        z_ln_ready = sem("z_ln_ready")
        bias_ready = sem("bias_ready")
        h_mm = sem("h_mm")
        gelu_done = sem("gelu_done")
        scores_ready = sem("scores_ready")
        exp_done = sem("exp_done")
        mask_done = sem("mask_done")
        head_added = sem("head_added")
        g_ready = sem("g_ready")
        gT_mm = sem("gT_mm")
        gT_ready = sem("gT_ready")
        out_mm = sem("out_mm")
        x_updated = sem("x_updated")
        avar_ready = sem("avar_ready")
        ascale_ready = sem("ascale_ready")
        xl_ready = sem("xl_ready")
        xlT_mm = sem("xlT_mm")
        xlT_ready = sem("xlT_ready")
        t_mm = sem("t_mm")
        t_ready = sem("t_ready")
        att_scores = sem("att_scores")
        neg_max_ready = sem("neg_max_ready")
        att_exp = sem("att_exp")
        a_ready = sem("a_ready")
        aT_mm = sem("aT_mm")
        aT_ready = sem("aT_ready")
        yT_mm = sem("yT_mm")
        yT_ready = sem("yT_ready")
        o_mm = sem("o_mm")
        r_mm = sem("r_mm")
        r_ready = sem("r_ready")
        sq_ready = sem("sq_ready")
        mean_sq_ready = sem("mean_sq_ready")
        inv_rms_ready = sem("inv_rms_ready")
        att_added = sem("att_added")
        vector_step = sem("vector_step")
        stored = sem("stored")

        block = ctx.enter_context(nc.Block())

        def tile_of(n):
            if isinstance(n.j, int):
                v = n.value()
                if v < 4:
                    return v
                if v >= LAST - 3:
                    return TILES - 4 + v - (LAST - 3)
                j, k = (v - 4) // 4 + 1, (v - 4) % 4
                return 2 * (j + 1) + k if k < 2 else 2 * (j - 1) + k - 2
            d, k = n.b // 4, n.b % 4
            return (n.j + (d + 1)) * 2 + k if k < 2 else (n.j + (d - 1)) * 2 + (k - 2)

        def steps_of(j):
            if isinstance(j, int):
                if j <= 0:
                    return [(k, Count(0, 0, 2 * (j + 1) + k)) for k in range(2)]
                if j >= BATCHES - 1:
                    return [(k, Count(0, 0, LAST - 3 + 2 * (j - BATCHES + 1) + k)) for k in range(2)]
            return [(k, Count(j, 4, k)) for k in range(STEPS)]

        RUNS = [(0, 1), (2, 3), (4, LAST - 4), (LAST - 3, LAST - 2), (LAST - 1, LAST)]

        def in_run(n, d):
            if not isinstance(n.j, int):
                return True
            first, last = next(run for run in RUNS if run[0] <= n.value() <= run[1])
            return first <= n.value() + d <= last

        def attention_stages(j, units):
            if isinstance(j, int) and not 0 <= j < BATCHES:
                return [[] for _ in range(units)]
            todo = [[] for _ in range(32)]
            todo[0].append(("variance", None))
            todo[1].append(("normalize", None))
            for h in range(HEADS):
                for s in range(ATT_STAGES):
                    todo[min(HEAD_START[h] + s, 31)].append((s, h))
            if units == 32:
                return todo
            return [todo[2 * u] + todo[2 * u + 1] for u in range(units)]

        def split(stages):
            for i, (stage, _) in enumerate(stages):
                if stage in PE_STAGES:
                    return stages[:i + 1], stages[i + 1:]
            return stages, []

        def all_rounds(engine, one_round):
            for j in range(-1, LOOP[0]):
                one_round(j)
            with engine.Fori(LOOP[0], LOOP[1]) as j:
                one_round(j)
            for j in range(LOOP[1], BATCHES + 1):
                one_round(j)

        @block.sync
        def _(sp):
            sp.dma_start(wq16_sb[:, :, :], wq16).then_inc(sim_w_in, 16)
            sp.dma_start(keys_sb[:, :, :], keysT).then_inc(sim_w_in, 16)
            sp.dma_start(gamma_sb[:, :], gamma).then_inc(sim_w_in, 16)
            sp.dma_start(ident_sb[:, :], ident).then_inc(consts_in, 16)
            sp.dma_start(x_all[:, 0:4, :], x[:, 0:4, :]).then_inc(x_in, 16)
            sp.dma_start(select_f[:, :], select).then_inc(consts_in, 16)
            sp.dma_start(down[:, :], downT).then_inc(tables_in, 16)
            sp.dma_start(up_sb[:, :, :], up).then_inc(tables_in, 16)
            sp.dma_start(lamq_sb[:, :], lam_q).then_inc(lam_in, 16)
            sp.dma_start(lamk_sb[:, :], lam_k).then_inc(lam_in, 16)
            sp.dma_start(wqa_sb[:, :, :], wq_a).then_inc(att_w_in, 16)
            sp.dma_start(wka_sb[:, :, :], wk_a).then_inc(att_w_in, 16)
            sp.dma_start(wva_sb[:, :, :], wv_a).then_inc(att_w_in, 16)
            sp.dma_start(woT_sb[:, :, :], woT).then_inc(att_w_in, 16)
            sp.dma_start(rms_sb[:, :], rms).then_inc(att_w_in, 16)
            sp.dma_start(wn_sb[:, :, 0:2 * P], wvT).then_inc(att_w_in, 16)
            sp.dma_start(x_all[:, 4:TILES, :], x[:, 4:TILES, :]).then_inc(x_in, 16)
            with sp.Fori(0, BATCHES - 2) as b:
                sp.wait_ge(x_updated, b * 4 + 8)
                sp.dma_start(out[:, bass.ds(b * 2, 2), :], x_all[:, bass.ds(b * 2, 2), :]).then_inc(stored, 16)
            for b in range(BATCHES - 2, BATCHES):
                sp.wait_ge(x_updated, LAST + 1 - 2 * (BATCHES - 1 - b))
                sp.dma_start(out[:, 2 * b:2 * b + 2, :], x_all[:, 2 * b:2 * b + 2, :]).then_inc(stored, 16)
            sp.wait_ge(stored, 16 * BATCHES)

        @block.tensor
        def _(pe):
            mm = nc.tensor.matmul
            misc_reader = [None]
            att_m_reader = [None]

            def misc_free(reader):
                if misc_reader[0]:
                    reach(pe, *misc_reader[0])
                misc_reader[0] = reader

            def att_m_free(reader):
                if att_m_reader[0]:
                    reach(pe, *att_m_reader[0])
                att_m_reader[0] = reader

            def sum_scores(n, h):
                g = n * UNITS + h
                if h == 0:
                    reach(pe, lowT_ready, n + 1)
                if h == 2:
                    reach(pe, gelu_done, n + 1)
                else:
                    reach(pe, mask_done, g - 1)
                r = 64 * (h % 2)
                for q in range(2):
                    half = slice(q * 512, (q + 1) * 512)
                    mm(s_ps[:, h % 2, half], high_midT[:, n.odd(), h, :], select_sb[:, half],
                       start=True, stop=False)
                for q in range(2):
                    half = slice(q * 512, (q + 1) * 512)
                    last = mm(s_ps[:, h % 2, half], lowT[r:r + 64, n.odd(), h // 2, :],
                              select_sb[r:r + 64, half], start=False, stop=True)
                last.then_inc(scores_ready, 1)

            def z_transpose(m):
                reach(pe, z_ready, m + 1)
                misc_free((zT_ready, m + 1))
                nc.tensor.transpose(misc[:, 0:P], z[:, :], ident_sb[:, :]).then_inc(zT_mm, 1)

            def similarities(m):
                misc_free((sim_ready, m + 1))
                mm(misc[:, 0:512], zT[:, m.odd(), :], w_sim[:, :], start=True, stop=True).then_inc(sim_mm, 1)

            def high_transpose(m):
                reach(pe, parts_ready, m + 1)
                misc_free((highT_ready, m + 1))
                for h in range(HEADS):
                    last = nc.tensor.transpose(misc_b[:, h * P:(h + 1) * P],
                                               high_mid[:, h, :, :].rearrange("p a k -> p (a k)"), ident_b[:, :])
                last.then_inc(highT_mm, 1)

            def low_transpose(m):
                misc_free((lowT_ready, m + 1))
                for c in range(HEADS // 2):
                    last = nc.tensor.transpose(misc_b[:, c * P:(c + 1) * P],
                                               low[:, 2 * c:2 * c + 2, :].rearrange("p a k -> p (a k)"),
                                               ident_b[:, :])
                last.then_inc(lowT_mm, 1)

            def expert_inputs(n):
                reach(pe, mask_done, n * UNITS + 1)
                for q in range(2):
                    half = slice(q * 512, (q + 1) * 512)
                    last = mm(s_ps[:, 0, half], zT[:, n.odd(), :], down[:, half], start=True, stop=True)
                last.then_inc(h_mm, 1)

            def g_transpose(m, q):
                reach(pe, g_ready, m + 1)
                misc_free((gT_ready, m * 2 + q + 1))
                for c in range(4):
                    e = q * 512 + c * P
                    last = nc.tensor.transpose(misc[:, c * P:(c + 1) * P], g_buf[:, e:e + P], ident_sb[:, :])
                last.then_inc(gT_mm, 1)

            def expert_outputs(m):
                misc_free((x_updated, m + 1))
                for c in range(EXPERTS // P):
                    last = mm(misc[:, 0:P], gT[:, c * P:(c + 1) * P], up_sb[:, c, :],
                              start=(c == 0), stop=(c == EXPERTS // P - 1))
                last.then_inc(out_mm, 1)

            def attention(stage, j, h):
                a = Count(j, HEADS, h or 0)
                if stage == "normalize":
                    reach(pe, xl_ready, Count(j, 1, 1))
                    att_m_reader[0] = (r_ready, a)
                    att_m_free((xlT_ready, Count(j, 1, 1)))
                    for s in range(2):
                        last = nc.tensor.transpose(att_m[:, s * P:(s + 1) * P], xl[:, s, :], ident_sb[:, :])
                    last.then_inc(xlT_mm, 1)
                elif stage == 0:
                    reach(pe, xlT_ready, Count(j, 1, 1))
                    att_m_free((t_ready, a + 1))
                    for b in range(2):
                        last = mm(att_m[:, b * 256:(b + 1) * 256], m_sb[:, 2 * h + b, :], xlT[:, :],
                                  start=True, stop=True)
                    last.then_inc(t_mm, 1)
                elif stage == 1:
                    reach(pe, t_ready, a + 1)
                    reach(pe, att_exp, a)
                    for q in range(2):
                        for b in range(2):
                            last = mm(att_s[:, q, b * 256:(b + 1) * 256],
                                      t_sb[:, b * 256 + q * P:b * 256 + (q + 1) * P], xlT[:, :],
                                      start=True, stop=True)
                    last.then_inc(att_scores, 1)
                elif stage == 5:
                    reach(pe, a_ready, a + 1)
                    att_m_free((aT_ready, a + 1))
                    for k in range(2):
                        for q in range(2):
                            last = nc.tensor.transpose(att_m[:, k * 256 + q * P:k * 256 + (q + 1) * P],
                                                       a_att[:, q, k * P:(k + 1) * P], ident_sb[:, :])
                    last.then_inc(aT_mm, 1)
                elif stage == 6:
                    reach(pe, aT_ready, a + 1)
                    att_m_free((yT_ready, a + 1))
                    for k in range(2):
                        last = mm(att_m[:, 0:256], xl[:, k, :], aT[:, k, :], start=(k == 0), stop=(k == 1))
                    last.then_inc(yT_mm, 1)
                elif stage == 7:
                    reach(pe, yT_ready, a + 1)
                    att_m_free((sq_ready, a + 1))
                    for q in range(2):
                        last = mm(att_m[:, q * 256:(q + 1) * 256], yT[:, q * P:(q + 1) * P], wn_sb[:, h, 0:256],
                                  start=True, stop=True)
                    last.then_inc(o_mm, 1)
                elif stage == 8:
                    att_m_free((r_ready, a + 1))
                    for q in range(2):
                        last = mm(att_m[:, q * P:(q + 1) * P], yT[:, q * P:(q + 1) * P], wn_sb[:, h, 256:384],
                                  start=True, stop=True)
                    last.then_inc(r_mm, 1)

            pe.wait_ge(sim_w_in, 48)
            for g in range(2 * HEADS):
                h, p = g // 2, g % 2
                last = mm(misc[:, g * KEYS:(g + 1) * KEYS], wq16_sb[:, p * HEADS + h, :], keys_sb[:, g, :],
                          start=True, stop=True)
            last.then_inc(w_sim_mm, 1)
            pe.wait_ge(lam_mul, 1)
            pe.wait_ge(ones_set, 1)
            mm(att_m[:, 0:2 * HEADS], ones[:, :], lam_prod[:, :], start=True, stop=True).then_inc(lam_mm, 1)
            pe.wait_ge(att_w_in, 96)
            for g in range(2 * HEADS):
                last = mm(s_ps[:, g // 8, (g % 8) * P:(g % 8 + 1) * P], wqa_sb[:, g, :], wka_sb[:, g, :],
                          start=True, stop=True)
            last.then_inc(m_mm, 1)
            pe.wait_ge(wo_scaled, 1)
            for h in range(HEADS):
                for e in range(2):
                    last = mm(att_s[:, h // 4, (h % 4) * P:(h % 4 + 1) * P], wva_sb[:, 2 * h + e, :],
                              woT_sb[:, 2 * h + e, :], start=(e == 0), stop=(e == 1))
            last.then_inc(n_mm, 1)

            pe.wait_ge(consts_in, 32)
            pe.wait_ge(consts_b, 2)
            pe.wait_ge(tables_in, 32)
            pe.wait_ge(w_sim_ready, 2)
            pe.wait_ge(lam_exped, 1)
            pe.wait_ge(m_ready, 1)

            def begin(n):
                for m in (n, n + 1):
                    z_transpose(m)
                    similarities(m)
                high_transpose(n)
                low_transpose(n)
                sum_scores(n, 0)

            def one_round(j):
                steps = steps_of(j)
                stages = attention_stages(j, UNITS * len(steps))
                if isinstance(j, int) and j == 0:
                    pe.wait_ge(n_ready, 1)
                for k, n in steps:
                    if not in_run(n, -1):
                        begin(n)
                    misc_reader[0] = ((sim_ready, n + 2) if in_run(n, -1) and in_run(n, 1)
                                      else (lowT_ready, n + 1))
                    for u in range(UNITS):
                        first, others = split(stages[k * UNITS + u])
                        for stage, h in first:
                            attention(stage, j, h)
                        if u < UNITS - 1:
                            sum_scores(n, u + 1)
                        elif in_run(n, 1):
                            sum_scores(n + 1, 0)
                        for stage, h in others:
                            attention(stage, j, h)
                        if u == 0:
                            expert_inputs(n)
                        if u == 1 and in_run(n, 1):
                            high_transpose(n + 1)
                        if u in (2, 3) and in_run(n, -1):
                            g_transpose(n - 1, u - 2)
                        if u == 4 and in_run(n, -1):
                            expert_outputs(n - 1)
                        if u == 5 and in_run(n, 1):
                            low_transpose(n + 1)
                        if u == 6 and in_run(n, 2):
                            z_transpose(n + 2)
                        if u == 7 and in_run(n, 2):
                            similarities(n + 2)
                    if not in_run(n, 1):
                        g_transpose(n, 0)
                        g_transpose(n, 1)
                        expert_outputs(n)

            all_rounds(pe, one_round)

        @block.scalar
        def _(act):
            go = nc.scalar.activation

            def head_exp(n, h):
                g = n * UNITS + h
                if h == 0:
                    reach(act, bias_ready, n + 1)
                reach(act, scores_ready, g + 1)
                go(e_buf[:, h % 2, :], s_ps[:, h % 2, :], ACT.Exp,
                   bias=bias[:, n.odd(), h:h + 1]).then_inc(exp_done, 1)

            def copy_zT(m):
                reach(act, zT_mm, m + 1)
                go(zT[:, m.odd(), :], misc[:, 0:P], ACT.Copy).then_inc(zT_ready, 1)

            def copy_sim(m):
                reach(act, sim_mm, m + 1)
                go(sim[:, m.odd(), :, :].rearrange("p g k -> p (g k)"), misc[:, 0:512],
                   ACT.Copy).then_inc(sim_ready, 1)

            def high_part(m, transposed):
                reach(act, highT_mm, transposed)
                reach(act, sim_ready, m + 1)
                go(high_mid[:, :, 0, :], sim[:, m.odd(), :, :].rearrange("p (h a) k -> p h (a k)", a=2),
                   ACT.Copy).then_inc(high_ready, 1)

            def copy_highT(m):
                reach(act, highT_mm, m + 1)
                go(high_midT[:, m.odd(), :, :].rearrange("p h t -> p (h t)"), misc_b[:, :],
                   ACT.Copy).then_inc(highT_ready, 1)

            def copy_lowT(m):
                reach(act, lowT_mm, m + 1)
                go(lowT[:, m.odd(), :, :].rearrange("p c t -> p (c t)"), misc_b[:, 0:512],
                   ACT.Copy).then_inc(lowT_ready, 1)

            def gelu(n):
                reach(act, h_mm, n + 1)
                go(act_h[:, n.odd(), :], s_ps[:, 0, :], ACT.Gelu).then_inc(gelu_done, 1)
                act.preload_act_table_set("natural_log_exp_and_others")

            def copy_gT(m, q):
                reach(act, gT_mm, m * 2 + q + 1)
                go(gT[:, q * 512:(q + 1) * 512], misc[:, :], ACT.Copy).then_inc(gT_ready, 1)

            def best_exp(m):
                reach(act, best_d_ready, m + 1)
                go(best_e[:, :, :], best_d[:, :, :], ACT.Exp).then_inc(best_e_ready, 1)

            def best_ln(m):
                reach(act, z_sum_ready, m + 1)
                go(z_ln[:, :], z_sum[:, :], ACT.Ln).then_inc(z_ln_ready, 1)

            def attention(stage, j, h):
                a = Count(j, HEADS, h or 0)
                if stage == "normalize":
                    reach(act, xlT_mm, Count(j, 1, 1))
                    go(xlT[:, :], att_m[:, 0:256], ACT.Copy).then_inc(xlT_ready, 1)
                elif stage == 0:
                    reach(act, t_mm, a + 1)
                    go(t_sb[:, :], att_m[:, :], ACT.Copy).then_inc(t_ready, 1)
                elif stage == 3:
                    reach(act, neg_max_ready, a + 1)
                    for c in range(4):
                        q, b = c // 2, c % 2
                        last = go(e_att[:, c, :], att_s[:, q, b * 256:(b + 1) * 256], ACT.Exp,
                                  bias=neg_max[:, c:c + 1], scale=DIM_HEAD ** -0.5,
                                  accum_out=z_att[:, q, b:b + 1])
                    last.then_inc(att_exp, 1)
                elif stage == 5:
                    reach(act, aT_mm, a + 1)
                    go(aT[:, :, :].rearrange("p k q -> p (k q)"), att_m[:, :], ACT.Copy).then_inc(aT_ready, 1)
                elif stage == 6:
                    reach(act, yT_mm, a + 1)
                    go(yT[:, :], att_m[:, 0:256], ACT.Copy).then_inc(yT_ready, 1)
                elif stage == 7:
                    reach(act, o_mm, a + 1)
                    reach(act, mean_sq_ready, a)
                    for q in range(2):
                        last = go(squares[:, q, :], att_m[:, q * 256:(q + 1) * 256], ACT.Square,
                                  accum_out=sq_sum[:, q:q + 1])
                    last.then_inc(sq_ready, 1)
                elif stage == 8:
                    reach(act, r_mm, a + 1)
                    reach(act, att_added, a)
                    go(r_sb[:, :, :].rearrange("p q d -> p (q d)"), att_m[:, 0:256], ACT.Copy).then_inc(r_ready, 1)

            act.preload_act_table_set("natural_log_exp_and_others")
            act.wait_ge(lam_mm, 1)
            go(lam_exp[:, :, :].rearrange("p b h -> p (b h)"), att_m[:, 0:2 * HEADS],
               ACT.Exp).then_inc(lam_exped, 1)
            act.wait_ge(m_mm, 1)
            go(m_sb[:, :, :].rearrange("p g d -> p (g d)"), s_ps[:, :, :].rearrange("p s e -> p (s e)"),
               ACT.Copy).then_inc(m_ready, 1)
            act.wait_ge(n_mm, 1)
            go(wn_sb[:, :, 2 * P:3 * P], att_s[:, :, :].rearrange("p b (h d) -> p (b h) d", h=4),
               ACT.Copy).then_inc(n_ready, 1)

            def begin(n):
                for m in (n, n + 1):
                    copy_zT(m)
                    copy_sim(m)
                high_part(n, n)
                copy_highT(n)
                copy_lowT(n)
                best_exp(n)
                best_ln(n)
                head_exp(n, 0)

            def one_round(j):
                steps = steps_of(j)
                stages = attention_stages(j, UNITS * len(steps))
                for k, n in steps:
                    if not in_run(n, -1):
                        begin(n)
                        high_part(n + 1, n + 1)
                    for u in range(UNITS):
                        first, others = split(stages[k * UNITS + u])
                        if u == 6 and in_run(n, 1):
                            best_exp(n + 1)
                        for stage, h in first:
                            attention(stage, j, h)
                        if u < UNITS - 1:
                            head_exp(n, u + 1)
                        elif in_run(n, 1):
                            head_exp(n + 1, 0)
                        for stage, h in others:
                            attention(stage, j, h)
                        if u == 0:
                            gelu(n)
                        if u == 1 and in_run(n, 1):
                            copy_highT(n + 1)
                        if u in (2, 3) and in_run(n, -1):
                            copy_gT(n - 1, u - 2)
                        if u == 5 and in_run(n, 1):
                            copy_lowT(n + 1)
                        if u == 6 and in_run(n, 2):
                            copy_zT(n + 2)
                        if u == 6 and in_run(n, 1):
                            best_ln(n + 1)
                        if u == 7 and in_run(n, 2):
                            copy_sim(n + 2)
                            high_part(n + 2, n + 2)
                    if not in_run(n, 1):
                        copy_gT(n, 0)
                        copy_gT(n, 1)

            all_rounds(act, one_round)

        @block.gpsimd
        def _(pool):
            pool.memset(ones[:, :], 1.0).then_inc(ones_set, 1)
            pool.memset(minus_half[:, :], -0.5).then_inc(half_set, 1)
            pool.wait_ge(half_set, 1)

            def inverse_root(dst, src):
                return nc.gpsimd.tensor_tensor(dst, src, minus_half[:, 0:src.shape[1]], ALU.pow)

            def z_scale(m):
                reach(pool, var_ready, m + 1)
                inverse_root(scale[:, 2:3], scale[:, 1:2]).then_inc(scale_ready, 1)

            def parts(m):
                reach(pool, high_ready, m + 1)
                scores = sim[:, m.odd(), :, :].rearrange("p (h a) k -> p h (a k)", a=2)
                nc.gpsimd.tensor_tensor(rest_mid[:, :, :], scores, high_mid[:, :, 0, :],
                                        ALU.subtract).then_inc(parts_step, 1)
                nc.gpsimd.tensor_tensor(high_mid[:, :, 1, :], scores, high_mid[:, :, 0, :],
                                        ALU.subtract).then_inc(parts_step, 1)
                reach(pool, parts_step, m * 2 + 2)
                nc.gpsimd.tensor_tensor(low[:, :, :], rest_mid[:, :, :], high_mid[:, :, 1, :],
                                        ALU.subtract).then_inc(parts_ready, 1)

            def attention(stage, j, h):
                a = Count(j, HEADS, h or 0)
                if stage == "variance":
                    reach(pool, avar_ready, Count(j, 1, 1))
                    inverse_root(ascale[:, :], avar[:, :]).then_inc(ascale_ready, 1)
                elif stage == 8:
                    reach(pool, mean_sq_ready, a + 1)
                    inverse_root(inv_rms[:, :], mean_sq[:, :]).then_inc(inv_rms_ready, 1)

            def one_round(j):
                steps = steps_of(j)
                stages = attention_stages(j, UNITS * len(steps))
                for k, n in steps:
                    if not in_run(n, -1):
                        z_scale(n)
                        z_scale(n + 1)
                        parts(n)
                    for h in range(UNITS):
                        for stage, head in stages[k * UNITS + h]:
                            attention(stage, j, head)
                        added = n * (UNITS - 1) + (h - 1)
                        if h:
                            reach(pool, mask_done, n * UNITS + h + 1)
                            reach(pool, head_added, added)
                            nc.gpsimd.tensor_tensor(p_acc[:, n.odd(), :], p_acc[:, n.odd(), :],
                                                    w_buf[:, added.odd(), :],
                                                    ALU.add).then_inc(head_added, 1)
                        if h == 0 and in_run(n, 1):
                            parts(n + 1)
                        if h == 1 and in_run(n, 2):
                            z_scale(n + 2)
                    reach(pool, head_added, (n + 1) * (UNITS - 1))
                    reach(pool, gelu_done, n + 1)
                    reach(pool, gT_mm, n * 2)
                    nc.gpsimd.tensor_tensor(g_buf[:, :], p_acc[:, n.odd(), :], act_h[:, n.odd(), :],
                                            ALU.mult).then_inc(g_ready, 1)

            all_rounds(pool, one_round)

        @block.vector
        def _(dve):
            v = nc.vector
            made = [0]

            def step(ins):
                ins.then_inc(vector_step, 1)
                made[0] += 1
                return made[0]

            def use(number):
                dve.wait_ge(vector_step, number)

            def restart():
                dve.wait_ge(vector_step, made[0])
                dve.sem_clear(vector_step)
                made[0] = 0

            def x_rows(t):
                if isinstance(t, int):
                    return x_all[:, t, :]
                return x_all[:, bass.ds(t, 1), :].rearrange("p a d -> p (a d)")

            def variance(m, sims=0):
                use(step(v.bn_stats(out=stats[:, :], in_=x_rows(tile_of(m)))))
                use(step(v.bn_aggr(out=meanvar[:, :], in_=stats[:, :])))
                reach(dve, sim_ready, sims)
                use(step(v.tensor_scalar(scale[:, 0:1], meanvar[:, 1:2], EPS, NORM_FLOOR ** 2 / P,
                                         ALU.add, ALU.mult)))
                v.tensor_tensor(scale[:, 1:2], meanvar[:, 1:2], scale[:, 0:1], ALU.max).then_inc(var_ready, 1)

            def normalize(m):
                reach(dve, scale_ready, m + 1)
                reach(dve, zT_mm, m)
                v.tensor_scalar(z[:, :], x_rows(tile_of(m)), meanvar[:, 0:1], scale[:, 2:3],
                                ALU.subtract, ALU.mult).then_inc(z_ready, 1)

            def sort_scores(m, heads):
                groups = [(h, p) for h in heads for p in range(2)]
                done = [step(v.max(top[:, h, p, 0:8], sim[:, m.odd(), 2 * h + p, :])) for h, p in groups]
                for i, (h, p) in enumerate(groups):
                    use(done[i])
                    done[i] = step(v.match_replace(out=rest[:, 2 * h + p, :], in_to_replace=top[:, h, p, 0:8],
                                                   in_values=sim[:, m.odd(), 2 * h + p, :], imm_value=LOWEST))
                for i, (h, p) in enumerate(groups):
                    use(done[i])
                    done[i] = step(v.max(top[:, h, p, 8:16], rest[:, 2 * h + p, :]))
                return done[-1]

            def candidates(sorted_at):
                use(sorted_at)
                at = 0
                for a0, rows, cols in BLOCKS:
                    shape = [P, HEADS, rows, cols]
                    xs = top[:, :, 0, a0:a0 + rows].unsqueeze(3).to_broadcast(shape)
                    ys = top[:, :, 1, 0:cols].unsqueeze(2).to_broadcast(shape)
                    o = cands[:, :, at:at + rows * cols].rearrange("p h (a b) -> p h a b", a=rows)
                    done = step(v.tensor_tensor(o, xs, ys, ALU.add))
                    at += rows * cols
                return done

            def sort_candidates(heads, made_at):
                use(made_at)
                done = [step(v.max(best[:, h, 0:8], cands[:, h, :])) for h in heads]
                for i, h in enumerate(heads):
                    use(done[i])
                    done[i] = step(v.match_replace(out=cands_a[:, h, :], in_to_replace=best[:, h, 0:8],
                                                   in_values=cands[:, h, :], imm_value=LOWEST))
                for i, h in enumerate(heads):
                    use(done[i])
                    done[i] = step(v.max(best[:, h, 8:16], cands_a[:, h, :]))
                for i, h in enumerate(heads):
                    use(done[i])
                    done[i] = step(v.match_replace(out=cands_b[:, h, :], in_to_replace=best[:, h, 8:16],
                                                   in_values=cands_a[:, h, :], imm_value=LOWEST))
                return done[-1]

            def threshold(m, sorted_at):
                use(sorted_at)
                v.tensor_tensor(best_d[:, :, :], best[:, :, :],
                                best[:, :, 0:1].to_broadcast([P, HEADS, TOPK]),
                                ALU.subtract).then_inc(best_d_ready, 1)
                use(step(v.reduce_max(next_best[:, :], cands_b[:, :, :], AX.X)))
                use(step(v.tensor_tensor(next_best[:, :], next_best[:, :], best[:, :, TOPK - 1], ALU.add)))
                return step(v.tensor_scalar(thr[:, m.odd(), :], next_best[:, :], 0.5, None, ALU.mult))

            def sum_best(m):
                reach(dve, best_e_ready, m + 1)
                v.reduce_sum(z_sum[:, :], best_e[:, :, :], AX.X).then_inc(z_sum_ready, 1)

            def head_bias(m):
                reach(dve, z_ln_ready, m + 1)
                v.scalar_tensor_tensor(bias[:, m.odd(), :], z_ln[:, :], -1.0, best[:, :, 0],
                                       ALU.mult, ALU.subtract).then_inc(bias_ready, 1)

            def mask(n, h):
                g = n * UNITS + h
                reach(dve, exp_done, g + 1)
                if h == 0:
                    reach(dve, g_ready, n - 1)
                    dst = p_acc[:, n.odd(), :]
                else:
                    added = n * (UNITS - 1) + (h - 1)
                    reach(dve, head_added, added - 1)
                    dst = w_buf[:, added.odd(), :]
                v.scalar_tensor_tensor(dst, s_ps[:, h % 2, :], thr[:, n.odd(), h:h + 1],
                                       e_buf[:, h % 2, :], ALU.is_ge, ALU.mult).then_inc(mask_done, 1)

            def finish(m):
                reach(dve, out_mm, m + 1)
                xt = x_rows(tile_of(m))
                v.scalar_tensor_tensor(xt, misc[:, 0:P], 0.5, xt, ALU.mult, ALU.add).then_inc(x_updated, 1)

            def attention(stage, j, h, n):
                a = Count(j, HEADS, h or 0)
                if stage == "variance":
                    reach(dve, x_updated, n - 1 if in_run(n, -1) else n)
                    done = [step(v.bn_stats(out=astats[:, q, :], in_=x_rows(j * 2 + q))) for q in range(2)]
                    for q in range(2):
                        use(done[q])
                        done[q] = step(v.bn_aggr(out=ameanvar[:, q, :], in_=astats[:, q, :]))
                    use(done[1])
                    v.tensor_scalar(avar[:, :], ameanvar[:, :, 1], EPS, None, ALU.add).then_inc(avar_ready, 1)
                elif stage == "normalize":
                    reach(dve, ascale_ready, Count(j, 1, 1))
                    reach(dve, yT_mm, a)
                    for q in range(2):
                        last = v.tensor_scalar(xl[:, q, :], x_rows(j * 2 + q), ameanvar[:, q, 0:1],
                                               ascale[:, q:q + 1], ALU.subtract, ALU.mult)
                    last.then_inc(xl_ready, 1)
                elif stage == 2:
                    reach(dve, att_scores, a + 1)
                    use(step(v.reduce_max(row_max[:, :],
                                          att_s[:, :, :].rearrange("p q (b k) -> p (q b) k", b=2), AX.X)))
                    v.tensor_scalar(neg_max[:, :], row_max[:, :], -DIM_HEAD ** -0.5, None,
                                    ALU.mult).then_inc(neg_max_ready, 1)
                elif stage == 4:
                    reach(dve, att_exp, a + 1)
                    use(step(v.reciprocal(rz_att[:, h % 2, :, :], z_att[:, :, :])))
                    use(step(v.scalar_tensor_tensor(mix[:, :], z_att[:, :, 0], neg_lam[:, h:h + 1],
                                                    rz_att[:, h % 2, :, 1], ALU.mult, ALU.mult)))
                    reach(dve, aT_mm, a)
                    for q in range(2):
                        last = v.scalar_tensor_tensor(a_att[:, q, :], e_att[:, 2 * q + 1, :], mix[:, q:q + 1],
                                                      e_att[:, 2 * q, :], ALU.mult, ALU.add)
                    last.then_inc(a_ready, 1)
                elif stage == 8:
                    reach(dve, sq_ready, a + 1)
                    use(step(v.tensor_tensor(inv_a[:, :], sq_sum[:, :], rz_att[:, h % 2, :, 0], ALU.mult)))
                    use(step(v.scalar_tensor_tensor(inv_b[:, :], inv_a[:, :], 1.0 / (2 * DIM_HEAD),
                                                    rz_att[:, h % 2, :, 0], ALU.mult, ALU.mult)))
                    v.tensor_scalar(mean_sq[:, :], inv_b[:, :], EPS, None, ALU.add).then_inc(mean_sq_ready, 1)
                elif stage == 9:
                    reach(dve, inv_rms_ready, a + 1)
                    reach(dve, r_ready, a + 1)
                    use(step(v.tensor_tensor(out_scale[:, :], inv_rms[:, :], rz_att[:, h % 2, :, 0], ALU.mult)))
                    for q in range(2):
                        xt = x_rows(j * 2 + q)
                        last = v.scalar_tensor_tensor(xt, r_sb[:, q, :], out_scale[:, q:q + 1], xt,
                                                      ALU.mult, ALU.add)
                    last.then_inc(att_added, 1)

            dve.wait_ge(consts_in, 32)
            v.tensor_copy(select_sb[:, :], select_f[:, :]).then_inc(consts_b, 1)
            v.tensor_copy(ident_b[:, :], ident_sb[:, :]).then_inc(consts_b, 1)
            dve.wait_ge(lam_in, 32)
            v.tensor_tensor(lam_prod[:, :], lamq_sb[:, :], lamk_sb[:, :], ALU.mult).then_inc(lam_mul, 1)
            dve.wait_ge(w_sim_mm, 1)
            v.tensor_scalar(w_sim[:, :], misc[:, 0:512], gamma_sb[:, 0:1], None, ALU.mult).then_inc(w_sim_ready, 1)
            dve.wait_ge(tables_in, 32)
            v.tensor_scalar(down[:, :], down[:, :], gamma_sb[:, 0:1], None, ALU.mult).then_inc(w_sim_ready, 1)
            dve.wait_ge(lam_exped, 1)
            v.scalar_tensor_tensor(neg_lam[:, :], lam_exp[:, 1, :], -LAMBDA_INIT, lam_exp[:, 0, :],
                                   ALU.add, ALU.subtract)
            dve.wait_ge(att_w_in, 96)
            for e in range(2):
                wo_half = woT_sb[:, :, :].rearrange("p (h e) d -> p e h d", e=2)[:, e]
                last = v.tensor_scalar(wo_half, wo_half, rms_sb[:, e:e + 1], 1.0 - LAMBDA_INIT,
                                       ALU.mult, ALU.mult)
            last.then_inc(wo_scaled, 1)
            dve.wait_ge(x_in, 32)

            def begin(n):
                for m in (n, n + 1):
                    variance(m)
                    normalize(m)
                reach(dve, sim_ready, n + 1)
                at = sort_scores(n, range(HEADS))
                at = sort_candidates(range(HEADS), candidates(at))
                threshold(n, at)
                sum_best(n)
                head_bias(n)

            def one_round(j):
                steps = steps_of(j)
                stages = attention_stages(j, UNITS * len(steps))
                for k, n in steps:
                    if k == 0:
                        reach(dve, att_added, Count(j, HEADS, 0))
                    if not in_run(n, -1):
                        begin(n)
                    more = in_run(n, 1)
                    for u in range(UNITS):
                        late = []
                        if u == 7 and more:
                            head_bias(n + 1)
                        for stage, h in stages[k * UNITS + u]:
                            if stage == 9 and len(steps) == STEPS:
                                late.append((stage, h))
                            else:
                                attention(stage, j, h, n)
                        if u == 0 and more and not in_run(n, 2):
                            reach(dve, sim_ready, n + 2)
                        if u == 5 and in_run(n, 2):
                            normalize(n + 2)
                        if u == 5 and in_run(n, -1):
                            finish(n - 1)
                        mask(n, u)
                        for stage, h in late:
                            attention(stage, j, h, n)
                        if u == 0 and in_run(n, 2):
                            variance(n + 2, n + 2)
                        if more:
                            if u == 0:
                                sort_scores(n + 1, (0, 1, 2))
                            elif u == 1:
                                sort_scores(n + 1, (3, 4, 5))
                            elif u == 2:
                                cands_at = candidates(sort_scores(n + 1, (6, 7)))
                            elif u == 3:
                                sort_candidates(range(0, 4), cands_at)
                            elif u == 4:
                                sorted_at = sort_candidates(range(4, 8), cands_at)
                            elif u == 5:
                                threshold(n + 1, sorted_at)
                            elif u == 6:
                                sum_best(n + 1)
                    if not more:
                        finish(n)
                restart()

            restart()
            all_rounds(dve, one_round)


def kernel(**inputs):
    import numpy as np
    import concourse.bacc as bacc
    from concourse import mybir as mb
    from concourse.bass_utils import run_bass_kernel_spmd

    i = {k: np.asarray(a) for k, a in inputs.items()}
    X = i["L0_attn_X"]
    batches, seq, d = X.shape
    tiles = batches * seq // P
    split = lambda w: w.reshape(2 * HEADS, P, -1).transpose(1, 0, 2)
    col = np.arange(EXPERTS)
    row = np.arange(KEYS)[:, None]
    select = np.concatenate([col[None] // KEYS == row, col[None] % KEYS == row] * 2).astype(np.float32)
    arrays = {
        "x": X.reshape(tiles, P, d).transpose(1, 0, 2),
        "wq16": i["L0_ffn_wq"].reshape(2 * HEADS, 64, d).transpose(1, 0, 2),
        "keysT": i["L0_ffn_keys"].transpose(3, 0, 2, 1).reshape(64, 2 * HEADS, KEYS),
        "gamma": i["L0_ffn_gamma"].reshape(P, 1),
        "wq_a": split(i["L0_attn_Wq"]),
        "wk_a": split(i["L0_attn_Wk"]),
        "wv_a": split(i["L0_attn_Wv"]),
        "wvT": i["L0_attn_Wv"].T.reshape(P, HEADS, 2 * DIM_HEAD),
        "woT": split(i["L0_attn_Wo"].T),
        "rms": i["L0_attn_rms_scale"].reshape(2, P).T,
        "lam_q": np.concatenate([i["L0_attn_lambda_q1"], i["L0_attn_lambda_q2"]]).T,
        "lam_k": np.concatenate([i["L0_attn_lambda_k1"], i["L0_attn_lambda_k2"]]).T,
        "downT": i["L0_ffn_table_down"][:EXPERTS].T,
        "up": i["L0_ffn_table_up"][:EXPERTS].reshape(EXPERTS // P, P, d).transpose(1, 0, 2),
        "select": select,
        "ident": np.eye(P, dtype=np.float32),
    }
    arrays = {k: np.ascontiguousarray(a) for k, a in arrays.items()}
    nc = bacc.Bacc("TRN2", target_bir_lowering=False, num_devices=1)
    args = [nc.dram_tensor(k, a.shape, mb.dt.float32, kind="ExternalInput").ap() for k, a in arrays.items()]
    args.append(nc.dram_tensor("out", (P, tiles, d), mb.dt.float32, kind="ExternalOutput").ap())
    build(nc, *args)
    r = run_bass_kernel_spmd(nc, [arrays], core_ids=[0])
    got = r.results[0]["out"]
    return got.transpose(1, 0, 2).reshape(batches, seq, d)
```

```python
import math
from collections import namedtuple
from contextlib import ExitStack

import concourse.bass as bass
from concourse import mybir

F32 = mybir.dt.float32
BF16 = mybir.dt.bfloat16
ALU = mybir.AluOpType
ACT = mybir.ActivationFunctionType
AX = mybir.AxisListType

P = 128
HEADS = 8
DIM_HEAD = 128
KEYS = 32
EXPERTS = KEYS * KEYS
TOPK = 16
EPS = 1e-5
NORM_FLOOR = 1e-12
LAMBDA_INIT = 0.8 - 0.6 * math.exp(-0.3 * 1)
LOWEST = -3.0e38

BLOCKS = [(0, 1, 16), (1, 1, 8), (2, 2, 5), (4, 4, 3), (8, 8, 1)]
CANDS = sum(r * c for _, r, c in BLOCKS)

UNITS = 8
Step = namedtuple("Step", "main ahead1 ahead2 behind")
IDLE = Step(None, None, None, None)
GELU_UNIT = [0, 4, 0, 4]
HEAD_START = [2, 5, 8, 11, 14, 17, 20, 23]
ATT_STAGES = 10
PE_STAGES = ("normalize", 0, 1, 5, 6, 7, 8)
AFTER_MASK = (2, 4, 9)


class Count:

    def __init__(self, j, a, b):
        self.j, self.a, self.b = j, a, b

    def __add__(self, k):
        return Count(self.j, self.a, self.b + k)

    def __sub__(self, k):
        return self + (-k)

    def __mul__(self, k):
        return Count(self.j, self.a * k, self.b * k)

    def odd(self):
        assert self.a % 2 == 0
        return self.b % 2

    def value(self):
        if isinstance(self.j, int):
            return self.a * self.j + self.b
        return self.j * self.a + self.b if self.a else self.b


def reach(engine, sem, count):
    v = count.value() if isinstance(count, Count) else count
    if not isinstance(v, int) or v > 0:
        engine.wait_ge(sem, v)


def build(nc, x, wq16, keysT, gamma, wq_a, wk_a, wv_a, wvT, woT, rms, lam_q, lam_k, downT, up,
          select, ident, out):
    TILES = x.shape[1]
    BATCHES = TILES // 2
    LAST = TILES * 2 - 1
    LOOP = (2, BATCHES - 2)

    ctx = ExitStack()
    with ctx:
        def sb(name, shape, dt=F32):
            return ctx.enter_context(nc.sbuf_tensor(name, shape, dt))

        def ps(name, shape):
            return ctx.enter_context(nc.psum_tensor(name, shape, F32))

        def sem(name):
            return ctx.enter_context(nc.semaphore(name))

        x_all = sb("x_all", [P, TILES, P])
        wq16_sb = sb("wq16_sb", [64, 2 * HEADS, P])
        keys_sb = sb("keys_sb", [64, 2 * HEADS, KEYS])
        gamma_sb = sb("gamma_sb", [P, 1])
        w_sim = sb("w_sim", [P, 2 * HEADS * KEYS])
        down = sb("down", [P, EXPERTS])
        up_sb = sb("up_sb", [P, EXPERTS // P, P])
        select_f = sb("select_f", [P, EXPERTS])
        select_sb = sb("select_sb", [P, EXPERTS], BF16)
        ident_sb = sb("ident_sb", [P, P])
        ident_b = sb("ident_b", [P, P], BF16)
        ones = sb("ones", [P, P])
        wqa_sb = sb("wqa_sb", [P, 2 * HEADS, P])
        wka_sb = sb("wka_sb", [P, 2 * HEADS, P])
        wva_sb = sb("wva_sb", [P, 2 * HEADS, P])
        woT_sb = sb("woT_sb", [P, 2 * HEADS, P])
        rms_sb = sb("rms_sb", [P, 2])
        m_sb = sb("m_sb", [P, 2 * HEADS, P])
        wn_sb = sb("wn_sb", [P, HEADS, 3 * P])
        lamq_sb = sb("lamq_sb", [P, 2 * HEADS])
        lamk_sb = sb("lamk_sb", [P, 2 * HEADS])
        lam_prod = sb("lam_prod", [P, 2 * HEADS])
        lam_exp = sb("lam_exp", [P, 2, HEADS])
        neg_lam = sb("neg_lam", [P, HEADS])
        z = sb("z", [P, P])
        zT = sb("zT", [P, 2, P])
        sim = sb("sim", [P, 2, 2 * HEADS, KEYS])
        high_mid = sb("high_mid", [P, HEADS, 2, 2 * KEYS], BF16)
        rest_mid = sb("rest_mid", [P, HEADS, 2 * KEYS])
        low = sb("low", [P, HEADS, 2 * KEYS], BF16)
        high_midT = sb("high_midT", [P, 2, HEADS, P], BF16)
        lowT = sb("lowT", [P, 2, HEADS // 2, P], BF16)
        stats = sb("stats", [P, 6])
        meanvar = sb("meanvar", [P, 2])
        scale = sb("scale", [P, 3])
        minus_half = sb("minus_half", [P, 2])
        top = sb("top", [P, HEADS, 2, TOPK])
        rest = sb("rest", [P, 2 * HEADS, KEYS])
        cands = sb("cands", [P, HEADS, CANDS])
        cands_a = sb("cands_a", [P, HEADS, CANDS])
        cands_b = sb("cands_b", [P, HEADS, CANDS])
        best = sb("best", [P, HEADS, TOPK])
        best_d = sb("best_d", [P, HEADS, TOPK])
        best_e = sb("best_e", [P, HEADS, TOPK])
        next_best = sb("next_best", [P, HEADS])
        z_sum = sb("z_sum", [P, HEADS])
        z_ln = sb("z_ln", [P, HEADS])
        thr = sb("thr", [P, 2, HEADS])
        bias = sb("bias", [P, 2, HEADS])
        e_buf = sb("e_buf", [P, 2, EXPERTS])
        w_buf = sb("w_buf", [P, 2, EXPERTS])
        p_acc = sb("p_acc", [P, 2, EXPERTS])
        act_h = sb("act_h", [P, 2, EXPERTS])
        g_buf = sb("g_buf", [P, EXPERTS])
        gT = sb("gT", [P, EXPERTS])
        astats = sb("astats", [P, 2, 6])
        ameanvar = sb("ameanvar", [P, 2, 2])
        avar = sb("avar", [P, 2])
        ascale = sb("ascale", [P, 2])
        r_sb = sb("r_sb", [P, 2, P])
        xl = sb("xl", [P, 2, P])
        xlT = sb("xlT", [P, 2 * P])
        t_sb = sb("t_sb", [P, 4 * P])
        neg_max = sb("neg_max", [P, 4])
        e_att = sb("e_att", [P, 4, 2 * P])
        z_att = sb("z_att", [P, 2, 2])
        rz_att = sb("rz_att", [P, 2])
        eps_z = sb("eps_z", [P, 2, 2])
        mix = sb("mix", [P, 2])
        a_att = sb("a_att", [P, 2, 2 * P])
        aT = sb("aT", [P, 2, 2 * P])
        yT = sb("yT", [P, 2 * P])
        squares = sb("squares", [P, 2, 2 * P])
        sq_sum = sb("sq_sum", [P, 2])
        mean_sq = sb("mean_sq", [P, 2])
        out_scale = sb("out_scale", [P, 2])

        s_ps = ps("s_ps", [P, 2, EXPERTS])
        misc = ps("misc", [P, 512])
        misc_b = misc[:, :].bitcast(BF16)
        att_s = ps("att_s", [P, 2, 512])
        att_m = ps("att_m", [P, 512])

        x_first_in = sem("x_first_in")
        x_in = sem("x_in")
        sim_w_in = sem("sim_w_in")
        tables_in = sem("tables_in")
        consts_in = sem("consts_in")
        att_w_in = sem("att_w_in")
        lam_in = sem("lam_in")
        ones_set = sem("ones_set")
        consts_b = sem("consts_b")
        w_sim_mm = sem("w_sim_mm")
        w_sim_ready = sem("w_sim_ready")
        down_ready = sem("down_ready")
        lam_mul = sem("lam_mul")
        lam_mm = sem("lam_mm")
        lam_exped = sem("lam_exped")
        wo_scaled = sem("wo_scaled")
        m_mm = sem("m_mm")
        m_ready = sem("m_ready")
        n_mm = sem("n_mm")
        n_ready = sem("n_ready")
        half_set = sem("half_set")
        var_ready = sem("var_ready")
        scale_ready = sem("scale_ready")
        z_ready = sem("z_ready")
        zT_mm = sem("zT_mm")
        zT_ready = sem("zT_ready")
        sim_mm = sem("sim_mm")
        sim_ready = sem("sim_ready")
        high_ready = sem("high_ready")
        parts_step = sem("parts_step")
        parts_ready = sem("parts_ready")
        highT_mm = sem("highT_mm")
        highT_ready = sem("highT_ready")
        lowT_mm = sem("lowT_mm")
        lowT_ready = sem("lowT_ready")
        best_d_ready = sem("best_d_ready")
        best_e_ready = sem("best_e_ready")
        z_sum_ready = sem("z_sum_ready")
        z_ln_ready = sem("z_ln_ready")
        bias_ready = sem("bias_ready")
        h_mm = sem("h_mm")
        gelu_done = sem("gelu_done")
        scores_ready = sem("scores_ready")
        exp_done = sem("exp_done")
        mask_done = sem("mask_done")
        head_added = sem("head_added")
        g_ready = sem("g_ready")
        gT_mm = sem("gT_mm")
        gT_ready = sem("gT_ready")
        out_mm = sem("out_mm")
        x_updated = sem("x_updated")
        avar_ready = sem("avar_ready")
        ascale_ready = sem("ascale_ready")
        xl_ready = sem("xl_ready")
        xlT_mm = sem("xlT_mm")
        xlT_ready = sem("xlT_ready")
        t_mm = sem("t_mm")
        t_ready = sem("t_ready")
        att_scores = sem("att_scores")
        neg_max_ready = sem("neg_max_ready")
        att_exp = sem("att_exp")
        a_ready = sem("a_ready")
        aT_mm = sem("aT_mm")
        aT_ready = sem("aT_ready")
        yT_mm = sem("yT_mm")
        yT_ready = sem("yT_ready")
        o_mm = sem("o_mm")
        r_mm = sem("r_mm")
        r_ready = sem("r_ready")
        sq_ready = sem("sq_ready")
        mean_sq_ready = sem("mean_sq_ready")
        out_scale_ready = sem("out_scale_ready")
        att_added = sem("att_added")
        vector_step = sem("vector_step")
        stored = sem("stored")

        block = ctx.enter_context(nc.Block())

        def tile_of(n):
            if isinstance(n.j, int):
                v = n.value()
                if v < 4:
                    return v
                if v >= LAST - 3:
                    return TILES - 4 + v - (LAST - 3)
                j, k = (v - 4) // 4 + 1, (v - 4) % 4
                return 2 * (j + 1) + k if k < 2 else 2 * (j - 1) + k - 2
            d, k = n.b // 4, n.b % 4
            return (n.j + (d + 1)) * 2 + k if k < 2 else (n.j + (d - 1)) * 2 + (k - 2)

        RUNS = [(0, LAST - 4), (LAST - 3, LAST - 2), (LAST - 1, LAST)]

        def in_run(n, d):
            if isinstance(n.j, int):
                first, last = next(run for run in RUNS if run[0] <= n.value() <= run[1])
                if not first <= n.value() + d <= last:
                    return None
            return n + d

        def gelu_unit(n):
            return GELU_UNIT[n.b % 4]

        def full(n):
            return Step(n, in_run(n, 1), in_run(n, 2), in_run(n, -1))

        def begin(n):
            return [Step(None, None, n, n - 1 if n.b else None), Step(None, n, n + 1, None)]

        def steps_of(j):
            if isinstance(j, int):
                n = Count(0, 0, 2 * (j + 1) if j < 1 else LAST - 3 + 2 * (j - BATCHES + 1))
                if j == -1:
                    return begin(n) + [full(n), full(n + 1)]
                if j == 0:
                    return [full(n), full(n + 1), IDLE._replace(behind=n + 1), IDLE, IDLE]
                if j == 1:
                    n = Count(0, 0, 4)
                    return [full(n)._replace(behind=None)] + [full(n + k) for k in range(1, 4)]
                if j == BATCHES - 1:
                    return begin(n) + [full(n), full(n + 1)]
                if j == BATCHES:
                    return begin(n) + [full(n), full(n + 1), Step(None, None, None, n + 1)]
            return [full(Count(j, 4, k)) for k in range(4)]

        def ffn_done(j):
            return Count(j, 4, -2) if not isinstance(j, int) or j > 1 else 2 * (j + 1)

        def attention_stages(j):
            units = UNITS * len(steps_of(j))
            todo = [[] for _ in range(units)]
            if isinstance(j, int) and not 0 <= j < BATCHES:
                return todo
            late = 6 if isinstance(j, int) and j == 0 else 0
            todo[late].append(("variance", None))
            todo[late + 1].append(("normalize", None))
            for h in range(HEADS):
                for s in range(ATT_STAGES):
                    todo[min(HEAD_START[h] + s + late, units - 1)].append((s, h))
            return todo

        def units_of(j):
            stages = attention_stages(j)
            return [(*step, u, stages[k * UNITS + u])
                    for k, step in enumerate(steps_of(j)) for u in range(UNITS)]

        def weights_part(j, main, u):
            return u if isinstance(j, int) and j == 0 and main and main.b == 2 and u < 3 else None

        def split(stages):
            for i, (stage, _) in enumerate(stages):
                if stage in PE_STAGES:
                    return stages[:i + 1], stages[i + 1:]
            return stages, []

        def all_rounds(engine, one_round):
            for j in range(-1, LOOP[0]):
                one_round(j)
            with engine.Fori(LOOP[0], LOOP[1]) as j:
                one_round(j)
            for j in range(LOOP[1], BATCHES + 1):
                one_round(j)

        @block.sync
        def _(sp):
            sp.dma_start(wq16_sb[:, :, :], wq16).then_inc(sim_w_in, 16)
            sp.dma_start(keys_sb[:, :, :], keysT).then_inc(sim_w_in, 16)
            sp.dma_start(gamma_sb[:, :], gamma).then_inc(sim_w_in, 16)
            sp.dma_start(ident_sb[:, :], ident).then_inc(consts_in, 16)
            sp.dma_start(x_all[:, 0:4, :], x[:, 0:4, :]).then_inc(x_first_in, 16)
            sp.dma_start(select_f[:, :], select).then_inc(consts_in, 16)
            sp.dma_start(down[:, :], downT).then_inc(tables_in, 16)
            sp.dma_start(up_sb[:, :, :], up).then_inc(tables_in, 16)
            sp.dma_start(lamq_sb[:, :], lam_q).then_inc(lam_in, 16)
            sp.dma_start(lamk_sb[:, :], lam_k).then_inc(lam_in, 16)
            sp.dma_start(wqa_sb[:, :, :], wq_a).then_inc(att_w_in, 16)
            sp.dma_start(wka_sb[:, :, :], wk_a).then_inc(att_w_in, 16)
            sp.dma_start(wva_sb[:, :, :], wv_a).then_inc(att_w_in, 16)
            sp.dma_start(woT_sb[:, :, :], woT).then_inc(att_w_in, 16)
            sp.dma_start(rms_sb[:, :], rms).then_inc(att_w_in, 16)
            sp.dma_start(wn_sb[:, :, 0:2 * P], wvT).then_inc(att_w_in, 16)
            sp.dma_start(x_all[:, 4:TILES, :], x[:, 4:TILES, :]).then_inc(x_in, 16)
            with sp.Fori(0, BATCHES - 2) as b:
                sp.wait_ge(x_updated, b * 4 + 8)
                sp.dma_start(out[:, bass.ds(b * 2, 2), :], x_all[:, bass.ds(b * 2, 2), :]).then_inc(stored, 16)
            for b in range(BATCHES - 2, BATCHES):
                sp.wait_ge(x_updated, LAST + 1 - 2 * (BATCHES - 1 - b))
                sp.dma_start(out[:, 2 * b:2 * b + 2, :], x_all[:, 2 * b:2 * b + 2, :]).then_inc(stored, 16)
            sp.wait_ge(stored, 16 * BATCHES)

        @block.tensor
        def _(pe):
            mm = nc.tensor.matmul
            misc_reader = [None]
            att_m_reader = [None]

            def misc_free(reader):
                if misc_reader[0]:
                    reach(pe, *misc_reader[0])
                misc_reader[0] = reader

            def att_m_free(reader):
                if att_m_reader[0]:
                    reach(pe, *att_m_reader[0])
                att_m_reader[0] = reader

            def sum_scores(n, h):
                g = n * UNITS + h
                if h == 0:
                    reach(pe, lowT_ready, n + 1)
                if h == gelu_unit(n) + 2:
                    reach(pe, gelu_done, n + 1)
                else:
                    reach(pe, mask_done, g - 1)
                r = 64 * (h % 2)
                for q in range(2):
                    half = slice(q * 512, (q + 1) * 512)
                    mm(s_ps[:, h % 2, half], high_midT[:, n.odd(), h, :], select_sb[:, half],
                       start=True, stop=False)
                for q in range(2):
                    half = slice(q * 512, (q + 1) * 512)
                    last = mm(s_ps[:, h % 2, half], lowT[r:r + 64, n.odd(), h // 2, :],
                              select_sb[r:r + 64, half], start=False, stop=True)
                last.then_inc(scores_ready, 1)

            def z_transpose(m):
                reach(pe, z_ready, m + 1)
                misc_free((zT_ready, m + 1))
                nc.tensor.transpose(misc[:, 0:P], z[:, :], ident_sb[:, :]).then_inc(zT_mm, 1)

            def similarities(m):
                misc_free((sim_ready, m + 1))
                mm(misc[:, 0:512], zT[:, m.odd(), :], w_sim[:, :], start=True, stop=True).then_inc(sim_mm, 1)

            def high_transpose(m):
                reach(pe, parts_ready, m + 1)
                misc_free((highT_ready, m + 1))
                for h in range(HEADS):
                    last = nc.tensor.transpose(misc_b[:, h * P:(h + 1) * P],
                                               high_mid[:, h, :, :].rearrange("p a k -> p (a k)"), ident_b[:, :])
                last.then_inc(highT_mm, 1)

            def low_transpose(m):
                misc_free((lowT_ready, m + 1))
                for c in range(HEADS // 2):
                    last = nc.tensor.transpose(misc_b[:, c * P:(c + 1) * P],
                                               low[:, 2 * c:2 * c + 2, :].rearrange("p a k -> p (a k)"),
                                               ident_b[:, :])
                last.then_inc(lowT_mm, 1)

            def expert_inputs(n):
                u = gelu_unit(n)
                reach(pe, mask_done, n * UNITS + u + 1)
                for q in range(2):
                    half = slice(q * 512, (q + 1) * 512)
                    last = mm(s_ps[:, u % 2, half], zT[:, n.odd(), :], down[:, half], start=True, stop=True)
                last.then_inc(h_mm, 1)

            def g_transpose(m, q):
                reach(pe, g_ready, m + 1)
                misc_free((gT_ready, m * 2 + q + 1))
                for c in range(4):
                    e = q * 512 + c * P
                    last = nc.tensor.transpose(misc[:, c * P:(c + 1) * P], g_buf[:, e:e + P], ident_sb[:, :])
                last.then_inc(gT_mm, 1)

            def expert_outputs(m):
                misc_free((x_updated, m + 1))
                for c in range(EXPERTS // P):
                    last = mm(misc[:, 0:P], gT[:, c * P:(c + 1) * P], up_sb[:, c, :],
                              start=(c == 0), stop=(c == EXPERTS // P - 1))
                last.then_inc(out_mm, 1)

            def attention(stage, j, h):
                a = Count(j, HEADS, h or 0)
                if stage == "normalize":
                    if isinstance(j, int) and j == 0:
                        pe.wait_ge(n_ready, 1)
                    reach(pe, xl_ready, Count(j, 1, 1))
                    att_m_reader[0] = (r_ready, a)
                    att_m_free((xlT_ready, Count(j, 1, 1)))
                    for s in range(2):
                        last = nc.tensor.transpose(att_m[:, s * P:(s + 1) * P], xl[:, s, :], ident_sb[:, :])
                    last.then_inc(xlT_mm, 1)
                elif stage == 0:
                    reach(pe, xlT_ready, Count(j, 1, 1))
                    att_m_free((t_ready, a + 1))
                    for b in range(2):
                        last = mm(att_m[:, b * 256:(b + 1) * 256], m_sb[:, 2 * h + b, :], xlT[:, :],
                                  start=True, stop=True)
                    last.then_inc(t_mm, 1)
                elif stage == 1:
                    reach(pe, t_ready, a + 1)
                    reach(pe, att_exp, a)
                    for q in range(2):
                        for b in range(2):
                            last = mm(att_s[:, q, b * 256:(b + 1) * 256],
                                      t_sb[:, b * 256 + q * P:b * 256 + (q + 1) * P], xlT[:, :],
                                      start=True, stop=True)
                    last.then_inc(att_scores, 1)
                elif stage == 5:
                    reach(pe, a_ready, a + 1)
                    att_m_free((aT_ready, a + 1))
                    for k in range(2):
                        for q in range(2):
                            last = nc.tensor.transpose(att_m[:, k * 256 + q * P:k * 256 + (q + 1) * P],
                                                       a_att[:, q, k * P:(k + 1) * P], ident_sb[:, :])
                    last.then_inc(aT_mm, 1)
                elif stage == 6:
                    reach(pe, aT_ready, a + 1)
                    att_m_free((yT_ready, a + 1))
                    for k in range(2):
                        last = mm(att_m[:, 0:256], xl[:, k, :], aT[:, k, :], start=(k == 0), stop=(k == 1))
                    last.then_inc(yT_mm, 1)
                elif stage == 7:
                    reach(pe, yT_ready, a + 1)
                    att_m_free((sq_ready, a + 1))
                    for q in range(2):
                        last = mm(att_m[:, q * 256:(q + 1) * 256], yT[:, q * P:(q + 1) * P], wn_sb[:, h, 0:256],
                                  start=True, stop=True)
                    last.then_inc(o_mm, 1)
                elif stage == 8:
                    att_m_free((r_ready, a + 1))
                    for q in range(2):
                        last = mm(att_m[:, q * P:(q + 1) * P], yT[:, q * P:(q + 1) * P], wn_sb[:, h, 256:384],
                                  start=True, stop=True)
                    last.then_inc(r_mm, 1)

            pe.wait_ge(sim_w_in, 48)
            for g in range(2 * HEADS):
                h, p = g // 2, g % 2
                last = mm(misc[:, g * KEYS:(g + 1) * KEYS], wq16_sb[:, p * HEADS + h, :], keys_sb[:, g, :],
                          start=True, stop=True)
            last.then_inc(w_sim_mm, 1)
            pe.wait_ge(consts_in, 32)
            pe.wait_ge(consts_b, 2)
            pe.wait_ge(w_sim_ready, 1)

            def attention_weights(part):
                if part == 0:
                    pe.wait_ge(lam_mul, 1)
                    pe.wait_ge(ones_set, 1)
                    mm(att_m[:, 0:2 * HEADS], ones[:, :], lam_prod[:, :], start=True, stop=True).then_inc(lam_mm, 1)
                    pe.wait_ge(att_w_in, 96)
                if part == 1:
                    pe.wait_ge(m_ready, 1)
                if part < 2:
                    for g in range(HEADS):
                        last = mm(att_s[:, g // 4, (g % 4) * P:(g % 4 + 1) * P], wqa_sb[:, part * HEADS + g, :],
                                  wka_sb[:, part * HEADS + g, :], start=True, stop=True)
                    last.then_inc(m_mm, 1)
                else:
                    pe.wait_ge(wo_scaled, 1)
                    pe.wait_ge(m_ready, 2)
                    for h in range(HEADS):
                        for e in range(2):
                            last = mm(att_s[:, h // 4, (h % 4) * P:(h % 4 + 1) * P], wva_sb[:, 2 * h + e, :],
                                      woT_sb[:, 2 * h + e, :], start=(e == 0), stop=(e == 1))
                    last.then_inc(n_mm, 1)
                    pe.wait_ge(lam_exped, 1)

            def one_round(j):
                if not isinstance(j, int) or j == LOOP[1]:
                    misc_reader[0] = (sim_ready, steps_of(j)[0].ahead1 + 1)
                for main, ahead1, ahead2, behind, u, stages in units_of(j):
                    first, others = split(stages)
                    for stage, h in first:
                        attention(stage, j, h)
                    if u < UNITS - 1 and main:
                        sum_scores(main, u + 1)
                    if u == UNITS - 1 and ahead1:
                        sum_scores(ahead1, 0)
                    for stage, h in others:
                        attention(stage, j, h)
                    if u == 1 and ahead1:
                        high_transpose(ahead1)
                    if u in (2, 3) and behind:
                        g_transpose(behind, u - 2)
                    if u == 4 and behind:
                        expert_outputs(behind)
                    if u == 5 and ahead1:
                        low_transpose(ahead1)
                    if u == 6 and ahead2:
                        z_transpose(ahead2)
                    if u == 7 and ahead2:
                        similarities(ahead2)
                    if main and u == gelu_unit(main):
                        if isinstance(j, int) and j == -1:
                            pe.wait_ge(down_ready, 1)
                        expert_inputs(main)
                    if weights_part(j, main, u) is not None:
                        attention_weights(weights_part(j, main, u))

            all_rounds(pe, one_round)

        @block.scalar
        def _(act):
            go = nc.scalar.activation

            def head_exp(n, h):
                g = n * UNITS + h
                if h == 0:
                    reach(act, bias_ready, n + 1)
                reach(act, scores_ready, g + 1)
                go(e_buf[:, h % 2, :], s_ps[:, h % 2, :], ACT.Exp,
                   bias=bias[:, n.odd(), h:h + 1]).then_inc(exp_done, 1)

            def copy_zT(m):
                reach(act, zT_mm, m + 1)
                go(zT[:, m.odd(), :], misc[:, 0:P], ACT.Copy).then_inc(zT_ready, 1)

            def copy_sim(m):
                reach(act, sim_mm, m + 1)
                go(sim[:, m.odd(), :, :].rearrange("p g k -> p (g k)"), misc[:, 0:512],
                   ACT.Copy).then_inc(sim_ready, 1)

            def high_part(m):
                reach(act, highT_mm, m)
                reach(act, sim_ready, m + 1)
                go(high_mid[:, :, 0, :], sim[:, m.odd(), :, :].rearrange("p (h a) k -> p h (a k)", a=2),
                   ACT.Copy).then_inc(high_ready, 1)

            def copy_highT(m):
                reach(act, highT_mm, m + 1)
                go(high_midT[:, m.odd(), :, :].rearrange("p h t -> p (h t)"), misc_b[:, :],
                   ACT.Copy).then_inc(highT_ready, 1)

            def copy_lowT(m):
                reach(act, lowT_mm, m + 1)
                go(lowT[:, m.odd(), :, :].rearrange("p c t -> p (c t)"), misc_b[:, 0:512],
                   ACT.Copy).then_inc(lowT_ready, 1)

            def gelu(n):
                reach(act, h_mm, n + 1)
                go(act_h[:, n.odd(), :], s_ps[:, gelu_unit(n) % 2, :], ACT.Gelu).then_inc(gelu_done, 1)
                act.preload_act_table_set("natural_log_exp_and_others")

            def copy_gT(m, q):
                reach(act, gT_mm, m * 2 + q + 1)
                go(gT[:, q * 512:(q + 1) * 512], misc[:, :], ACT.Copy).then_inc(gT_ready, 1)

            def best_exp(m):
                reach(act, best_d_ready, m + 1)
                go(best_e[:, :, :], best_d[:, :, :], ACT.Exp).then_inc(best_e_ready, 1)

            def best_ln(m):
                reach(act, z_sum_ready, m + 1)
                go(z_ln[:, :], z_sum[:, :], ACT.Ln).then_inc(z_ln_ready, 1)

            def attention(stage, j, h):
                a = Count(j, HEADS, h or 0)
                if stage == "normalize":
                    reach(act, xlT_mm, Count(j, 1, 1))
                    go(xlT[:, :], att_m[:, 0:256], ACT.Copy).then_inc(xlT_ready, 1)
                elif stage == 0:
                    reach(act, t_mm, a + 1)
                    go(t_sb[:, :], att_m[:, :], ACT.Copy).then_inc(t_ready, 1)
                elif stage == 3:
                    reach(act, neg_max_ready, a + 1)
                    for c in range(4):
                        q, b = c // 2, c % 2
                        last = go(e_att[:, c, :], att_s[:, q, b * 256:(b + 1) * 256], ACT.Exp,
                                  bias=neg_max[:, c:c + 1],
                                  accum_out=z_att[:, q, b:b + 1])
                    last.then_inc(att_exp, 1)
                elif stage == 5:
                    reach(act, aT_mm, a + 1)
                    go(aT[:, :, :].rearrange("p k q -> p (k q)"), att_m[:, :], ACT.Copy).then_inc(aT_ready, 1)
                elif stage == 6:
                    reach(act, yT_mm, a + 1)
                    go(yT[:, :], att_m[:, 0:256], ACT.Copy).then_inc(yT_ready, 1)
                elif stage == 7:
                    reach(act, o_mm, a + 1)
                    reach(act, mean_sq_ready, a)
                    for q in range(2):
                        last = go(squares[:, q, :], att_m[:, q * 256:(q + 1) * 256], ACT.Square,
                                  accum_out=sq_sum[:, q:q + 1])
                    last.then_inc(sq_ready, 1)
                elif stage == 8:
                    reach(act, r_mm, a + 1)
                    reach(act, att_added, a)
                    go(r_sb[:, :, :].rearrange("p q d -> p (q d)"), att_m[:, 0:256], ACT.Copy).then_inc(r_ready, 1)

            act.preload_act_table_set("natural_log_exp_and_others")

            def attention_weights(part):
                if part == 0:
                    act.wait_ge(lam_mm, 1)
                    go(lam_exp[:, :, :].rearrange("p b h -> p (b h)"), att_m[:, 0:2 * HEADS],
                       ACT.Exp).then_inc(lam_exped, 1)
                if part < 2:
                    act.wait_ge(m_mm, part + 1)
                    go(m_sb[:, part * HEADS:(part + 1) * HEADS, :].rearrange("p g d -> p (g d)"),
                       att_s[:, :, :].rearrange("p b c -> p (b c)"), ACT.Copy,
                       scale=DIM_HEAD ** -0.5).then_inc(m_ready, 1)
                else:
                    act.wait_ge(n_mm, 1)
                    go(wn_sb[:, :, 2 * P:3 * P], att_s[:, :, :].rearrange("p b (h d) -> p (b h) d", h=4),
                       ACT.Copy).then_inc(n_ready, 1)

            def one_round(j):
                for main, ahead1, ahead2, behind, u, stages in units_of(j):
                    first, others = split(stages)
                    if u == 6 and ahead1:
                        best_exp(ahead1)
                    for stage, h in first:
                        attention(stage, j, h)
                    if u < UNITS - 1 and main:
                        head_exp(main, u + 1)
                    if u == UNITS - 1 and ahead1:
                        head_exp(ahead1, 0)
                    for stage, h in sorted(others, key=lambda at: at[0] == 3):
                        attention(stage, j, h)
                    if u == 1 and ahead1:
                        copy_highT(ahead1)
                    if u in (2, 3) and behind:
                        copy_gT(behind, u - 2)
                    if u == 5 and ahead1:
                        copy_lowT(ahead1)
                    if u == 6 and ahead2:
                        copy_zT(ahead2)
                    if u == 6 and ahead1:
                        best_ln(ahead1)
                    if u == 7 and ahead2:
                        copy_sim(ahead2)
                        high_part(ahead2)
                    if main and u == gelu_unit(main):
                        gelu(main)
                    if weights_part(j, main, u) is not None:
                        attention_weights(weights_part(j, main, u))

            all_rounds(act, one_round)

        @block.gpsimd
        def _(pool):
            pool.memset(ones[:, :], 1.0).then_inc(ones_set, 1)
            pool.memset(minus_half[:, :], -0.5).then_inc(half_set, 1)
            pool.wait_ge(half_set, 1)

            def inverse_root(dst, src):
                return nc.gpsimd.tensor_tensor(dst, src, minus_half[:, 0:src.shape[1]], ALU.pow)

            def z_scale(m):
                reach(pool, var_ready, m + 1)
                inverse_root(scale[:, 2:3], scale[:, 1:2]).then_inc(scale_ready, 1)

            def parts(m):
                reach(pool, high_ready, m + 1)
                scores = sim[:, m.odd(), :, :].rearrange("p (h a) k -> p h (a k)", a=2)
                nc.gpsimd.tensor_tensor(rest_mid[:, :, :], scores, high_mid[:, :, 0, :],
                                        ALU.subtract).then_inc(parts_step, 1)
                nc.gpsimd.tensor_tensor(high_mid[:, :, 1, :], scores, high_mid[:, :, 0, :],
                                        ALU.subtract).then_inc(parts_step, 1)
                reach(pool, parts_step, m * 2 + 2)
                nc.gpsimd.tensor_tensor(low[:, :, :], rest_mid[:, :, :], high_mid[:, :, 1, :],
                                        ALU.subtract).then_inc(parts_ready, 1)

            def attention(stage, j, h):
                a = Count(j, HEADS, h or 0)
                if stage == "variance":
                    reach(pool, avar_ready, Count(j, 1, 1))
                    inverse_root(ascale[:, :], avar[:, :]).then_inc(ascale_ready, 1)
                elif stage == 8:
                    reach(pool, mean_sq_ready, a + 1)
                    inverse_root(out_scale[:, :], mean_sq[:, :]).then_inc(out_scale_ready, 1)

            def add_head(n, h):
                added = n * (UNITS - 1) + (h - 1)
                reach(pool, mask_done, n * UNITS + h + 1)
                reach(pool, head_added, added)
                nc.gpsimd.tensor_tensor(p_acc[:, n.odd(), :], p_acc[:, n.odd(), :],
                                        w_buf[:, added.odd(), :], ALU.add).then_inc(head_added, 1)

            def weigh(n):
                reach(pool, head_added, (n + 1) * (UNITS - 1))
                reach(pool, gelu_done, n + 1)
                reach(pool, gT_mm, n * 2)
                nc.gpsimd.tensor_tensor(g_buf[:, :], p_acc[:, n.odd(), :], act_h[:, n.odd(), :],
                                        ALU.mult).then_inc(g_ready, 1)

            def one_round(j):
                for main, ahead1, ahead2, behind, u, stages in units_of(j):
                    for stage, h in stages:
                        attention(stage, j, h)
                    if u > 0 and main:
                        add_head(main, u)
                    if u == 0 and ahead1:
                        parts(ahead1)
                    if u == 1 and ahead2:
                        z_scale(ahead2)
                    if u == 7 and main:
                        weigh(main)

            all_rounds(pool, one_round)

        @block.vector
        def _(dve):
            v = nc.vector
            made = [0]

            def step(ins):
                ins.then_inc(vector_step, 1)
                made[0] += 1
                return made[0]

            def use(number):
                dve.wait_ge(vector_step, number)

            def restart():
                dve.wait_ge(vector_step, made[0])
                dve.sem_clear(vector_step)
                made[0] = 0

            def x_rows(t):
                if isinstance(t, int):
                    return x_all[:, t, :]
                return x_all[:, bass.ds(t, 1), :].rearrange("p a d -> p (a d)")

            def variance(sims):
                use(step(v.bn_aggr(out=meanvar[:, :], in_=stats[:, :])))
                reach(dve, sim_ready, sims)
                return step(v.tensor_scalar(scale[:, 0:1], meanvar[:, 1:2], EPS, NORM_FLOOR ** 2 / P,
                                            ALU.add, ALU.mult))

            def floor_variance(floor_at):
                use(floor_at)
                v.tensor_tensor(scale[:, 1:2], meanvar[:, 1:2], scale[:, 0:1], ALU.max).then_inc(var_ready, 1)

            def normalize(m):
                reach(dve, scale_ready, m + 1)
                reach(dve, zT_mm, m)
                v.tensor_scalar(z[:, :], x_rows(tile_of(m)), meanvar[:, 0:1], scale[:, 2:3],
                                ALU.subtract, ALU.mult).then_inc(z_ready, 1)

            def sort_scores(m, heads):
                groups = [(h, p) for h in heads for p in range(2)]
                done = [step(v.max(top[:, h, p, 0:8], sim[:, m.odd(), 2 * h + p, :])) for h, p in groups]
                for i, (h, p) in enumerate(groups):
                    use(done[i])
                    done[i] = step(v.match_replace(out=rest[:, 2 * h + p, :], in_to_replace=top[:, h, p, 0:8],
                                                   in_values=sim[:, m.odd(), 2 * h + p, :], imm_value=LOWEST))
                for i, (h, p) in enumerate(groups):
                    use(done[i])
                    done[i] = step(v.max(top[:, h, p, 8:16], rest[:, 2 * h + p, :]))
                return done[-1]

            def candidates(sorted_at):
                use(sorted_at)
                at = 0
                for a0, rows, cols in BLOCKS:
                    shape = [P, HEADS, rows, cols]
                    xs = top[:, :, 0, a0:a0 + rows].unsqueeze(3).to_broadcast(shape)
                    ys = top[:, :, 1, 0:cols].unsqueeze(2).to_broadcast(shape)
                    o = cands[:, :, at:at + rows * cols].rearrange("p h (a b) -> p h a b", a=rows)
                    done = step(v.tensor_tensor(o, xs, ys, ALU.add))
                    at += rows * cols
                return done

            def sort_candidates(heads, made_at):
                use(made_at)
                done = [step(v.max(best[:, h, 0:8], cands[:, h, :])) for h in heads]
                for i, h in enumerate(heads):
                    use(done[i])
                    done[i] = step(v.match_replace(out=cands_a[:, h, :], in_to_replace=best[:, h, 0:8],
                                                   in_values=cands[:, h, :], imm_value=LOWEST))
                for i, h in enumerate(heads):
                    use(done[i])
                    done[i] = step(v.max(best[:, h, 8:16], cands_a[:, h, :]))
                for i, h in enumerate(heads):
                    use(done[i])
                    done[i] = step(v.match_replace(out=cands_b[:, h, :], in_to_replace=best[:, h, 8:16],
                                                   in_values=cands_a[:, h, :], imm_value=LOWEST))
                return done[-1]

            def threshold(m, sorted_at):
                use(sorted_at)
                v.tensor_tensor(best_d[:, :, :], best[:, :, :],
                                best[:, :, 0:1].to_broadcast([P, HEADS, TOPK]),
                                ALU.subtract).then_inc(best_d_ready, 1)
                use(step(v.reduce_max(next_best[:, :], cands_b[:, :, :], AX.X)))
                use(step(v.tensor_tensor(next_best[:, :], next_best[:, :], best[:, :, TOPK - 1], ALU.add)))
                return step(v.tensor_scalar(thr[:, m.odd(), :], next_best[:, :], 0.5, None, ALU.mult))

            def sum_best(m):
                reach(dve, best_e_ready, m + 1)
                v.reduce_sum(z_sum[:, :], best_e[:, :, :], AX.X).then_inc(z_sum_ready, 1)

            def head_bias(m):
                reach(dve, z_ln_ready, m + 1)
                v.scalar_tensor_tensor(bias[:, m.odd(), :], z_ln[:, :], -1.0, best[:, :, 0],
                                       ALU.mult, ALU.subtract).then_inc(bias_ready, 1)

            def mask(n, h):
                g = n * UNITS + h
                reach(dve, exp_done, g + 1)
                if h == 0:
                    reach(dve, g_ready, n - 1)
                    dst = p_acc[:, n.odd(), :]
                else:
                    added = n * (UNITS - 1) + (h - 1)
                    reach(dve, head_added, added - 1)
                    dst = w_buf[:, added.odd(), :]
                v.scalar_tensor_tensor(dst, s_ps[:, h % 2, :], thr[:, n.odd(), h:h + 1],
                                       e_buf[:, h % 2, :], ALU.is_ge, ALU.mult).then_inc(mask_done, 1)

            def finish(m):
                reach(dve, out_mm, m + 1)
                xt = x_rows(tile_of(m))
                v.scalar_tensor_tensor(xt, misc[:, 0:P], 0.5, xt, ALU.mult, ALU.add).then_inc(x_updated, 1)

            def attention(stage, j, h):
                a = Count(j, HEADS, h or 0)
                if stage == "variance":
                    reach(dve, x_updated, ffn_done(j))
                    done = [step(v.bn_stats(out=astats[:, q, :], in_=x_rows(j * 2 + q))) for q in range(2)]
                    for q in range(2):
                        use(done[q])
                        done[q] = step(v.bn_aggr(out=ameanvar[:, q, :], in_=astats[:, q, :]))
                    use(done[1])
                    v.tensor_scalar(avar[:, :], ameanvar[:, :, 1], EPS, None, ALU.add).then_inc(avar_ready, 1)
                elif stage == "normalize":
                    reach(dve, ascale_ready, Count(j, 1, 1))
                    reach(dve, yT_mm, a)
                    for q in range(2):
                        last = v.tensor_scalar(xl[:, q, :], x_rows(j * 2 + q), ameanvar[:, q, 0:1],
                                               ascale[:, q:q + 1], ALU.subtract, ALU.mult)
                    last.then_inc(xl_ready, 1)
                elif stage == 2:
                    reach(dve, att_scores, a + 1)
                    v.reduce_max(neg_max[:, :], att_s[:, :, :].rearrange("p q (b k) -> p (q b) k", b=2), AX.X,
                                 negate=True).then_inc(neg_max_ready, 1)
                elif stage == 4:
                    reach(dve, att_exp, a + 1)
                    inverted = step(v.reciprocal(rz_att[:, :], z_att[:, :, 1]))
                    v.scalar_tensor_tensor(eps_z[:, h % 2, :], z_att[:, :, 0], EPS, z_att[:, :, 0],
                                           ALU.mult, ALU.mult)
                    use(inverted)
                    use(step(v.scalar_tensor_tensor(mix[:, :], z_att[:, :, 0], neg_lam[:, h:h + 1],
                                                    rz_att[:, :], ALU.mult, ALU.mult)))
                    reach(dve, aT_mm, a)
                    for q in range(2):
                        last = v.scalar_tensor_tensor(a_att[:, q, :], e_att[:, 2 * q + 1, :], mix[:, q:q + 1],
                                                      e_att[:, 2 * q, :], ALU.mult, ALU.add)
                    last.then_inc(a_ready, 1)
                elif stage == 8:
                    reach(dve, sq_ready, a + 1)
                    v.scalar_tensor_tensor(mean_sq[:, :], sq_sum[:, :], 1.0 / (2 * DIM_HEAD),
                                           eps_z[:, h % 2, :], ALU.mult, ALU.add).then_inc(mean_sq_ready, 1)
                elif stage == 9:
                    reach(dve, out_scale_ready, a + 1)
                    reach(dve, r_ready, a + 1)
                    for q in range(2):
                        xt = x_rows(j * 2 + q)
                        last = v.scalar_tensor_tensor(xt, r_sb[:, q, :], out_scale[:, q:q + 1], xt,
                                                      ALU.mult, ALU.add)
                    last.then_inc(att_added, 1)

            dve.wait_ge(consts_in, 32)
            v.tensor_copy(select_sb[:, :], select_f[:, :]).then_inc(consts_b, 1)
            v.tensor_copy(ident_b[:, :], ident_sb[:, :]).then_inc(consts_b, 1)
            dve.wait_ge(w_sim_mm, 1)
            v.tensor_scalar(w_sim[:, :], misc[:, 0:512], gamma_sb[:, 0:1], None, ALU.mult).then_inc(w_sim_ready, 1)
            dve.wait_ge(x_first_in, 16)

            def scale_down():
                dve.wait_ge(tables_in, 32)
                v.tensor_scalar(down[:, :], down[:, :], gamma_sb[:, 0:1], None, ALU.mult).then_inc(down_ready, 1)

            def lambda_products():
                dve.wait_ge(lam_in, 32)
                v.tensor_tensor(lam_prod[:, :], lamq_sb[:, :], lamk_sb[:, :], ALU.mult).then_inc(lam_mul, 1)

            def attention_weights():
                dve.wait_ge(lam_exped, 1)
                v.scalar_tensor_tensor(neg_lam[:, :], lam_exp[:, 1, :], -LAMBDA_INIT, lam_exp[:, 0, :],
                                       ALU.add, ALU.subtract)
                dve.wait_ge(att_w_in, 96)
                for e in range(2):
                    wo_half = woT_sb[:, :, :].rearrange("p (h e) d -> p e h d", e=2)[:, e]
                    last = v.tensor_scalar(wo_half, wo_half, rms_sb[:, e:e + 1], 1.0 - LAMBDA_INIT,
                                           ALU.mult, ALU.mult)
                last.then_inc(wo_scaled, 1)

            def one_round(j):
                reach(dve, att_added, Count(j, HEADS, 0))
                if isinstance(j, int) and j == 0:
                    dve.wait_ge(x_in, 16)
                for main, ahead1, ahead2, behind, u, stages in units_of(j):
                    if isinstance(j, int) and j == -1 and ahead1 and not main and u == 1:
                        scale_down()
                    if weights_part(j, main, u) == 0:
                        lambda_products()
                    if weights_part(j, main, u) == 1:
                        attention_weights()
                    if u == 7 and ahead1:
                        head_bias(ahead1)
                    if u == 0 and ahead1 and not ahead2:
                        reach(dve, sim_ready, ahead1 + 1)
                    if u == 0 and main:
                        mask(main, 0)
                    for stage, h in stages:
                        if stage not in AFTER_MASK:
                            attention(stage, j, h)
                    if u == 5 and ahead2:
                        normalize(ahead2)
                    if u == 5 and behind:
                        finish(behind)
                    if u > 0 and main:
                        mask(main, u)
                    if u == 0 and ahead2:
                        stats_at = step(v.bn_stats(out=stats[:, :], in_=x_rows(tile_of(ahead2))))
                    for stage, h in stages:
                        if stage in AFTER_MASK:
                            attention(stage, j, h)
                    if u == 0 and ahead2:
                        use(stats_at)
                        floor_at = variance(ahead1 + 1 if ahead1 else 0)
                    if ahead1:
                        if u == 0:
                            sort_scores(ahead1, (0, 1, 2))
                        if u == 1:
                            sort_scores(ahead1, (3, 4, 5))
                        if u == 2:
                            cands_at = candidates(sort_scores(ahead1, (6, 7)))
                        if u == 3:
                            sort_candidates(range(0, 4), cands_at)
                        if u == 4:
                            sorted_at = sort_candidates(range(4, 8), cands_at)
                        if u == 5:
                            threshold(ahead1, sorted_at)
                        if u == 6:
                            sum_best(ahead1)
                    if u == 0 and ahead2:
                        floor_variance(floor_at)
                restart()

            restart()
            all_rounds(dve, one_round)


def kernel(**inputs):
    import numpy as np
    import concourse.bacc as bacc
    from concourse import mybir as mb
    from concourse.bass_utils import run_bass_kernel_spmd

    i = {k: np.asarray(a) for k, a in inputs.items()}
    X = i["L0_attn_X"]
    batches, seq, d = X.shape
    tiles = batches * seq // P
    split = lambda w: w.reshape(2 * HEADS, P, -1).transpose(1, 0, 2)
    col = np.arange(EXPERTS)
    row = np.arange(KEYS)[:, None]
    select = np.concatenate([col[None] // KEYS == row, col[None] % KEYS == row] * 2).astype(np.float32)
    arrays = {
        "x": X.reshape(tiles, P, d).transpose(1, 0, 2),
        "wq16": i["L0_ffn_wq"].reshape(2 * HEADS, 64, d).transpose(1, 0, 2),
        "keysT": i["L0_ffn_keys"].transpose(3, 0, 2, 1).reshape(64, 2 * HEADS, KEYS),
        "gamma": i["L0_ffn_gamma"].reshape(P, 1),
        "wq_a": split(i["L0_attn_Wq"]),
        "wk_a": split(i["L0_attn_Wk"]),
        "wv_a": split(i["L0_attn_Wv"]),
        "wvT": i["L0_attn_Wv"].T.reshape(P, HEADS, 2 * DIM_HEAD),
        "woT": split(i["L0_attn_Wo"].T),
        "rms": i["L0_attn_rms_scale"].reshape(2, P).T,
        "lam_q": np.concatenate([i["L0_attn_lambda_q1"], i["L0_attn_lambda_q2"]]).T,
        "lam_k": np.concatenate([i["L0_attn_lambda_k1"], i["L0_attn_lambda_k2"]]).T,
        "downT": i["L0_ffn_table_down"][:EXPERTS].T,
        "up": i["L0_ffn_table_up"][:EXPERTS].reshape(EXPERTS // P, P, d).transpose(1, 0, 2),
        "select": select,
        "ident": np.eye(P, dtype=np.float32),
    }
    arrays = {k: np.ascontiguousarray(a) for k, a in arrays.items()}
    nc = bacc.Bacc("TRN2", target_bir_lowering=False, num_devices=1)
    args = [nc.dram_tensor(k, a.shape, mb.dt.float32, kind="ExternalInput").ap() for k, a in arrays.items()]
    args.append(nc.dram_tensor("out", (P, tiles, d), mb.dt.float32, kind="ExternalOutput").ap())
    build(nc, *args)
    r = run_bass_kernel_spmd(nc, [arrays], core_ids=[0])
    got = r.results[0]["out"]
    return got.transpose(1, 0, 2).reshape(batches, seq, d)
```
